# Optimizing a Trainium2 kernel written in Bass

```python
import numpy as np
import jax
import jax.numpy as jnp

def _softmax(x, axis=-1):
    return jax.nn.softmax(x, axis=axis)

def _gelu(x):
    return jax.nn.gelu(x, approximate=True)

def _silu(x):
    return jax.nn.silu(x)

def _sigmoid(x):
    return jax.nn.sigmoid(x)

def _layernorm(x, axis=-1, eps=1e-05):
    m = jnp.mean(x, axis=axis, keepdims=True)
    v = jnp.var(x, axis=axis, keepdims=True)
    return (x - m) / jnp.sqrt(v + eps)

def _scatter_add(tgt, idx, src, axis=0):
    return tgt.at[idx].add(src)

def _segment_sum(src, seg, n):
    return jax.ops.segment_sum(src, seg, n)
kernel_name = 'mk_adaln_ffn_d2_seqx_r8_01d22b'

def setup_inputs(seed: int=0):
    np.random.seed(seed)
    _w = jnp.asarray

    def _rec_inputs():
        import jax
        import jax.numpy as jnp
        _rk = jax.random.key(seed)
        x = -0.000125 + 0.9999 * jax.random.normal(jax.random.fold_in(_rk, 1), (16, 128, 128), jnp.float32)
        _lenS = 128 - jax.random.randint(jax.random.fold_in(_rk, 7), (16,), 0, max(1, 128 // 4) + 1, jnp.int32)
        _lenS2 = 128 - jax.random.randint(jax.random.fold_in(_rk, 8), (16,), 0, max(1, 128 // 4) + 1, jnp.int32)
        cond_1024 = -0.00493535 + 1.00056 * jax.random.normal(jax.random.fold_in(_rk, 11), (16, 128), jnp.float32)
        return (x, cond_1024)
    x, cond_1024 = _rec_inputs()

    def _L0_cond_setup():
        import jax, jax.numpy as jnp
        import numpy as np
        key = jax.random.key(seed)
        k1, k2, k3, k4 = jax.random.split(key, 4)
        N, T, D, H = (64, 64, 128, 128)
        x = jax.random.normal(k1, (N, T, D), dtype=jnp.float32)
        h0 = jax.random.normal(k2, (N, H), dtype=jnp.float32)
        Wx = jax.random.normal(k3, (D, 4 * H), dtype=jnp.float32) / np.sqrt(D)
        Wh = jax.random.normal(k4, (H, 4 * H), dtype=jnp.float32) / np.sqrt(H)
        b = jnp.zeros((4 * H,), dtype=jnp.float32)
        return {'x': x, 'h0': h0, 'Wx': Wx, 'Wh': Wh, 'b': b}
    _L0_cond_all = _L0_cond_setup()
    _L0_cond_in = {k: v for k, v in _L0_cond_all.items() if k in ('Wx', 'Wh', 'b')}
    del _L0_cond_all

    def _L0_ffn_setup():
        import jax, jax.numpy as jnp
        import numpy as np
        D_MODEL = 128
        NUM_TILES = 64
        TPC = 8
        NUM_CLUSTERS = NUM_TILES // TPC
        GRID = 16
        COMP_H = 32
        NUM_KNOTS = 8
        EPS_LN = 1e-05

        def _calibrate(scores, knots, temperature):
            K = knots.shape[0]
            normalized = jax.nn.sigmoid(scores / (temperature[0] + 1e-06))
            idx_float = normalized * (K - 1)
            idx_low = jnp.clip(idx_float.astype(jnp.int32), 0, K - 2)
            idx_high = idx_low + 1
            t = idx_float - idx_low.astype(scores.dtype)
            val_low = knots[idx_low]
            val_high = knots[idx_high]
            return val_low + t * (val_high - val_low)

        def _forward(x, signatures_raw, knot_values, temperature, compress_w1, compress_b1, compress_w2, compress_b2, spline_w1, spline_b1, spline_w2, spline_b2, directions, norm_gamma, norm_beta, output_scale):
            B, T, D = x.shape
            xf = x.reshape(-1, D)
            q = jnp.where(signatures_raw > 0.3, 1.0, jnp.where(signatures_raw < -0.3, -1.0, 0.0)).astype(signatures_raw.dtype)
            sigs = signatures_raw + jax.lax.stop_gradient(q - signatures_raw)
            cluster_sigs = jnp.sign(sigs.reshape(NUM_CLUSTERS, TPC, D).mean(axis=1))
            cluster_scores = xf @ cluster_sigs.T
            cluster_gates = _calibrate(cluster_scores, knot_values, temperature)
            cluster_idx = jnp.argmax(cluster_gates, axis=-1)
            tile_scores = xf @ sigs.T
            tile_gates = _calibrate(tile_scores, knot_values, temperature)
            gates_by_cluster = tile_gates.reshape(-1, NUM_CLUSTERS, TPC)
            sel_gates = jnp.take_along_axis(gates_by_cluster, cluster_idx[:, None, None], axis=1)[:, 0, :]
            local_idx = jnp.argmax(sel_gates, axis=-1)
            tile_idx = cluster_idx * TPC + local_idx
            h = jax.nn.gelu(xf @ compress_w1 + compress_b1, approximate=False)
            comp = jnp.tanh(h @ compress_w2 + compress_b2)
            w1 = spline_w1[tile_idx]
            b1 = spline_b1[tile_idx]
            hh = jax.nn.relu(jnp.einsum('ni,nig->ng', comp, w1) + b1)
            w2 = spline_w2[tile_idx]
            b2 = spline_b2[tile_idx]
            mag = jnp.einsum('ng,ngo->no', hh, w2) + b2
            ffn_out = mag * directions[tile_idx] * output_scale[0]
            y = xf + ffn_out
            mu = y.mean(axis=-1, keepdims=True)
            var = ((y - mu) ** 2).mean(axis=-1, keepdims=True)
            y = (y - mu) / jnp.sqrt(var + EPS_LN) * norm_gamma + norm_beta
            return y.reshape(B, T, D)
        key = jax.random.key(seed)
        ks = jax.random.split(key, 12)
        B, T = (4, 512)
        x = jax.random.normal(ks[0], (B, T, D_MODEL), dtype=jnp.float32)
        signatures_raw = jax.random.normal(ks[1], (NUM_TILES, D_MODEL), dtype=jnp.float32) * 0.5
        knot_values = jax.nn.sigmoid(jnp.linspace(-3.0, 3.0, NUM_KNOTS).astype(jnp.float32))
        temperature = jnp.ones((1,), dtype=jnp.float32)
        compress_w1 = jax.random.normal(ks[2], (D_MODEL, COMP_H), dtype=jnp.float32) * (1.0 / np.sqrt(D_MODEL))
        compress_b1 = jnp.zeros((COMP_H,), dtype=jnp.float32)
        compress_w2 = jax.random.normal(ks[3], (COMP_H, 2), dtype=jnp.float32) * (1.0 / np.sqrt(COMP_H))
        compress_b2 = jnp.zeros((2,), dtype=jnp.float32)
        spline_w1 = jax.random.normal(ks[4], (NUM_TILES, 2, GRID), dtype=jnp.float32) * (1.0 / np.sqrt(2.0))
        spline_b1 = jnp.zeros((NUM_TILES, GRID), dtype=jnp.float32)
        spline_w2 = jax.random.normal(ks[5], (NUM_TILES, GRID, 1), dtype=jnp.float32) * (1.0 / np.sqrt(GRID))
        spline_b2 = jnp.zeros((NUM_TILES, 1), dtype=jnp.float32)
        directions = jax.random.normal(ks[6], (NUM_TILES, D_MODEL), dtype=jnp.float32) * 0.02
        norm_gamma = jnp.ones((D_MODEL,), dtype=jnp.float32)
        norm_beta = jnp.zeros((D_MODEL,), dtype=jnp.float32)
        output_scale = jnp.ones((1,), dtype=jnp.float32) * 0.1
        return dict(x=x, signatures_raw=signatures_raw, knot_values=knot_values, temperature=temperature, compress_w1=compress_w1, compress_b1=compress_b1, compress_w2=compress_w2, compress_b2=compress_b2, spline_w1=spline_w1, spline_b1=spline_b1, spline_w2=spline_w2, spline_b2=spline_b2, directions=directions, norm_gamma=norm_gamma, norm_beta=norm_beta, output_scale=output_scale)
    _L0_ffn_all = _L0_ffn_setup()
    _L0_ffn_in = {k: v for k, v in _L0_ffn_all.items() if k in ('signatures_raw', 'knot_values', 'temperature', 'compress_w1', 'compress_b1', 'compress_w2', 'compress_b2', 'spline_w1', 'spline_b1', 'spline_w2', 'spline_b2', 'directions', 'norm_gamma', 'norm_beta', 'output_scale')}
    del _L0_ffn_all

    def _L1_cond_setup():
        import jax, jax.numpy as jnp
        import numpy as np
        N, T, D, H = (64, 64, 128, 128)
        key = jax.random.key(seed)
        k1, k2, k3, k4 = jax.random.split(key, 4)
        x = jax.random.normal(k1, (N, T, D), dtype=jnp.float32)
        h0 = jax.random.normal(k2, (N, H), dtype=jnp.float32)
        Wx = jax.random.normal(k3, (D, 4 * H), dtype=jnp.float32) / np.sqrt(D)
        Wh = jax.random.normal(k4, (H, 4 * H), dtype=jnp.float32) / np.sqrt(H)
        b = jnp.zeros((4 * H,), dtype=jnp.float32)
        return {'x': x, 'h0': h0, 'Wx': Wx, 'Wh': Wh, 'b': b}
    _L1_cond_all = _L1_cond_setup()
    _L1_cond_in = {k: v for k, v in _L1_cond_all.items() if k in ('Wx', 'Wh', 'b')}
    del _L1_cond_all

    def _L1_ffn_setup():
        import jax, jax.numpy as jnp
        import numpy as np
        D_MODEL = 128
        M = 64
        INNER = 16
        key = jax.random.key(seed)
        ks = jax.random.split(key, 9)

        def init(k, shape, fan_in):
            bound = 1.0 / np.sqrt(fan_in)
            return jax.random.uniform(k, shape, jnp.float32, -bound, bound)
        x = jax.random.normal(ks[0], (16, 512, D_MODEL), dtype=jnp.float32)
        Win = init(ks[1], (D_MODEL, M), D_MODEL)
        bin_ = init(ks[2], (M,), D_MODEL)
        W1 = init(ks[3], (M, INNER), 1)
        b1 = init(ks[4], (M, INNER), 1)
        W2 = init(ks[5], (M, INNER), INNER)
        b2 = init(ks[6], (M,), INNER)
        Wout = init(ks[7], (M, D_MODEL), M)
        bout = init(ks[8], (D_MODEL,), M)
        return {'x': x, 'Win': Win, 'bin_': bin_, 'W1': W1, 'b1': b1, 'W2': W2, 'b2': b2, 'Wout': Wout, 'bout': bout}
    _L1_ffn_all = _L1_ffn_setup()
    _L1_ffn_in = {k: v for k, v in _L1_ffn_all.items() if k in ('Win', 'bin_', 'W1', 'b1', 'W2', 'b2', 'Wout', 'bout')}
    del _L1_ffn_all
    return {'x': x, 'cond_1024': cond_1024, 'L0_cond_Wx': _L0_cond_in['Wx'], 'L0_cond_Wh': _L0_cond_in['Wh'], 'L0_cond_b': _L0_cond_in['b'], 'L0_ffn_signatures_raw': _L0_ffn_in['signatures_raw'], 'L0_ffn_knot_values': _L0_ffn_in['knot_values'], 'L0_ffn_temperature': _L0_ffn_in['temperature'], 'L0_ffn_compress_w1': _L0_ffn_in['compress_w1'], 'L0_ffn_compress_b1': _L0_ffn_in['compress_b1'], 'L0_ffn_compress_w2': _L0_ffn_in['compress_w2'], 'L0_ffn_compress_b2': _L0_ffn_in['compress_b2'], 'L0_ffn_spline_w1': _L0_ffn_in['spline_w1'], 'L0_ffn_spline_b1': _L0_ffn_in['spline_b1'], 'L0_ffn_spline_w2': _L0_ffn_in['spline_w2'], 'L0_ffn_spline_b2': _L0_ffn_in['spline_b2'], 'L0_ffn_directions': _L0_ffn_in['directions'], 'L0_ffn_norm_gamma': _L0_ffn_in['norm_gamma'], 'L0_ffn_norm_beta': _L0_ffn_in['norm_beta'], 'L0_ffn_output_scale': _L0_ffn_in['output_scale'], 'L1_cond_Wx': _L1_cond_in['Wx'], 'L1_cond_Wh': _L1_cond_in['Wh'], 'L1_cond_b': _L1_cond_in['b'], 'L1_ffn_Win': _L1_ffn_in['Win'], 'L1_ffn_bin_': _L1_ffn_in['bin_'], 'L1_ffn_W1': _L1_ffn_in['W1'], 'L1_ffn_b1': _L1_ffn_in['b1'], 'L1_ffn_W2': _L1_ffn_in['W2'], 'L1_ffn_b2': _L1_ffn_in['b2'], 'L1_ffn_Wout': _L1_ffn_in['Wout'], 'L1_ffn_bout': _L1_ffn_in['bout']}

def reference(x, cond_1024, L0_cond_Wx, L0_cond_Wh, L0_cond_b, L0_ffn_signatures_raw, L0_ffn_knot_values, L0_ffn_temperature, L0_ffn_compress_w1, L0_ffn_compress_b1, L0_ffn_compress_w2, L0_ffn_compress_b2, L0_ffn_spline_w1, L0_ffn_spline_b1, L0_ffn_spline_w2, L0_ffn_spline_b2, L0_ffn_directions, L0_ffn_norm_gamma, L0_ffn_norm_beta, L0_ffn_output_scale, L1_cond_Wx, L1_cond_Wh, L1_cond_b, L1_ffn_Win, L1_ffn_bin_, L1_ffn_W1, L1_ffn_b1, L1_ffn_W2, L1_ffn_b2, L1_ffn_Wout, L1_ffn_bout):
    import jax
    import jax.numpy as jnp

    def _L0_cond_ref(x, h0, Wx, Wh, b):
        import jax, jax.numpy as jnp
        import numpy as np
        H = h0.shape[1]
        xW = jnp.einsum('ntd,dg->tng', x, Wx) + b

        def step(carry, xw_t):
            prev_h, prev_c = carry
            preact = xw_t + prev_h @ Wh
            i, f, o, g = jnp.split(preact, 4, axis=1)
            i = jax.nn.sigmoid(i)
            f = jax.nn.sigmoid(f)
            o = jax.nn.sigmoid(o)
            g = jnp.tanh(g)
            next_c = f * prev_c + i * g
            next_h = o * jnp.tanh(next_c)
            return ((next_h, next_c), next_h)
        c0 = jnp.zeros_like(h0)
        _, hs = jax.lax.scan(step, (h0, c0), xW)
        return jnp.transpose(hs, (1, 0, 2))

    def _L0_ffn_ref(x, signatures_raw, knot_values, temperature, compress_w1, compress_b1, compress_w2, compress_b2, spline_w1, spline_b1, spline_w2, spline_b2, directions, norm_gamma, norm_beta, output_scale):
        import jax, jax.numpy as jnp
        import numpy as np
        D_MODEL = 128
        NUM_TILES = 64
        TPC = 8
        NUM_CLUSTERS = NUM_TILES // TPC
        GRID = 16
        COMP_H = 32
        NUM_KNOTS = 8
        EPS_LN = 1e-05

        def _calibrate(scores, knots, temperature):
            K = knots.shape[0]
            normalized = jax.nn.sigmoid(scores / (temperature[0] + 1e-06))
            idx_float = normalized * (K - 1)
            idx_low = jnp.clip(idx_float.astype(jnp.int32), 0, K - 2)
            idx_high = idx_low + 1
            t = idx_float - idx_low.astype(scores.dtype)
            val_low = knots[idx_low]
            val_high = knots[idx_high]
            return val_low + t * (val_high - val_low)

        def _forward(x, signatures_raw, knot_values, temperature, compress_w1, compress_b1, compress_w2, compress_b2, spline_w1, spline_b1, spline_w2, spline_b2, directions, norm_gamma, norm_beta, output_scale):
            B, T, D = x.shape
            xf = x.reshape(-1, D)
            q = jnp.where(signatures_raw > 0.3, 1.0, jnp.where(signatures_raw < -0.3, -1.0, 0.0)).astype(signatures_raw.dtype)
            sigs = signatures_raw + jax.lax.stop_gradient(q - signatures_raw)
            cluster_sigs = jnp.sign(sigs.reshape(NUM_CLUSTERS, TPC, D).mean(axis=1))
            cluster_scores = xf @ cluster_sigs.T
            cluster_gates = _calibrate(cluster_scores, knot_values, temperature)
            cluster_idx = jnp.argmax(cluster_gates, axis=-1)
            tile_scores = xf @ sigs.T
            tile_gates = _calibrate(tile_scores, knot_values, temperature)
            gates_by_cluster = tile_gates.reshape(-1, NUM_CLUSTERS, TPC)
            sel_gates = jnp.take_along_axis(gates_by_cluster, cluster_idx[:, None, None], axis=1)[:, 0, :]
            local_idx = jnp.argmax(sel_gates, axis=-1)
            tile_idx = cluster_idx * TPC + local_idx
            h = jax.nn.gelu(xf @ compress_w1 + compress_b1, approximate=False)
            comp = jnp.tanh(h @ compress_w2 + compress_b2)
            w1 = spline_w1[tile_idx]
            b1 = spline_b1[tile_idx]
            hh = jax.nn.relu(jnp.einsum('ni,nig->ng', comp, w1) + b1)
            w2 = spline_w2[tile_idx]
            b2 = spline_b2[tile_idx]
            mag = jnp.einsum('ng,ngo->no', hh, w2) + b2
            ffn_out = mag * directions[tile_idx] * output_scale[0]
            y = xf + ffn_out
            mu = y.mean(axis=-1, keepdims=True)
            var = ((y - mu) ** 2).mean(axis=-1, keepdims=True)
            y = (y - mu) / jnp.sqrt(var + EPS_LN) * norm_gamma + norm_beta
            return y.reshape(B, T, D)
        return _forward(x, signatures_raw, knot_values, temperature, compress_w1, compress_b1, compress_w2, compress_b2, spline_w1, spline_b1, spline_w2, spline_b2, directions, norm_gamma, norm_beta, output_scale)

    def _L1_cond_ref(x, h0, Wx, Wh, b):
        import jax, jax.numpy as jnp
        import numpy as np
        N, T, D, H = (64, 64, 128, 128)
        Hdim = h0.shape[1]
        xW = jnp.einsum('ntd,dg->ntg', x, Wx) + b
        c0 = jnp.zeros_like(h0)

        def step(carry, xw_t):
            prev_h, prev_c = carry
            A = xw_t + prev_h @ Wh
            i = jax.nn.sigmoid(A[:, 0:Hdim])
            f = jax.nn.sigmoid(A[:, Hdim:2 * Hdim])
            o = jax.nn.sigmoid(A[:, 2 * Hdim:3 * Hdim])
            g = jnp.tanh(A[:, 3 * Hdim:4 * Hdim])
            next_c = f * prev_c + i * g
            next_h = o * jnp.tanh(next_c)
            return ((next_h, next_c), next_h)
        _, hs = jax.lax.scan(step, (h0, c0), jnp.swapaxes(xW, 0, 1))
        return jnp.swapaxes(hs, 0, 1)

    def _L1_ffn_ref(x, Win, bin_, W1, b1, W2, b2, Wout, bout):
        import jax, jax.numpy as jnp
        import numpy as np
        D_MODEL = 128
        M = 64
        INNER = 16
        s = jnp.einsum('btd,dm->btm', x, Win) + bin_
        h = jax.nn.relu(s[..., None] * W1 + b1)
        g = jnp.einsum('btmh,mh->btm', h, W2) + b2
        out = jnp.einsum('btm,md->btd', g, Wout) + bout
        return out
    x = x + _L0_ffn_ref(_L0_cond_ref(x, cond_1024, L0_cond_Wx, L0_cond_Wh, L0_cond_b), L0_ffn_signatures_raw, L0_ffn_knot_values, L0_ffn_temperature, L0_ffn_compress_w1, L0_ffn_compress_b1, L0_ffn_compress_w2, L0_ffn_compress_b2, L0_ffn_spline_w1, L0_ffn_spline_b1, L0_ffn_spline_w2, L0_ffn_spline_b2, L0_ffn_directions, L0_ffn_norm_gamma, L0_ffn_norm_beta, L0_ffn_output_scale)
    x = x + _L1_ffn_ref(_L1_cond_ref(x, cond_1024, L1_cond_Wx, L1_cond_Wh, L1_cond_b), L1_ffn_Win, L1_ffn_bin_, L1_ffn_W1, L1_ffn_b1, L1_ffn_W2, L1_ffn_b2, L1_ffn_Wout, L1_ffn_bout)
    return x

_drawn_inputs = setup_inputs


def setup_inputs(seed=0):
    import zlib

    import numpy as np

    out = dict(_drawn_inputs(seed))
    spreads = {'L0_cond_b': (0.0, 0.1),
     'L0_ffn_compress_b1': (0.0, 0.8),
     'L0_ffn_compress_b2': (0.0, 0.8),
     'L0_ffn_spline_b1': (0.0, 0.8),
     'L0_ffn_spline_b2': (0.0, 0.8),
     'L0_ffn_norm_gamma': (1.0, 0.2),
     'L0_ffn_norm_beta': (0.0, 0.1),
     'L1_cond_b': (0.0, 0.8)}
    factors = {'L0_ffn_signatures_raw': 8.0,
     'L0_ffn_knot_values': 8.0,
     'L0_ffn_compress_w1': 8.0,
     'L0_ffn_compress_w2': 8.0,
     'L0_ffn_spline_w1': 8.0,
     'L0_ffn_spline_w2': 8.0,
     'L0_ffn_directions': 8.0,
     'L1_cond_Wx': 4.947,
     'L1_cond_Wh': 8.0,
     'L1_ffn_Win': 4.875,
     'L1_ffn_bin_': 8.0,
     'L1_ffn_W1': 4.575}
    for name, (base, spread) in spreads.items():
        noise = np.random.default_rng([zlib.crc32(name.encode()), seed]).standard_normal(out[name].shape)
        drawn = base * np.exp(spread * noise) if base else spread * noise
        out[name] = jnp.asarray(drawn.astype(out[name].dtype))
    for name, factor in factors.items():
        out[name] = (out[name] * factor).astype(out[name].dtype)
    return out
```

```python
from contextlib import ExitStack

import numpy as np

import concourse.bass as bass
from concourse import mybir

ALU = mybir.AluOpType
ACT = mybir.ActivationFunctionType
F32 = mybir.dt.float32
BF16 = mybir.dt.bfloat16
AX_X = mybir.AxisListType.X

B, T, D = 16, 128, 128
STEPS = 8
TOK = STEPS * B
CHUNKS = T // STEPS
NT, NC, TPC = 64, 8, 8
KNOTS = 8
CH = 32
GRID = 16
M, INNER = 64, 16
HALF = INNER // 2
GATE = [2, 0, 1, 3]
EPS_LN = 1e-5

C_W1, C_B1, C_W2, C_B2, C_DIR = 0, 2 * GRID, 3 * GRID, 4 * GRID, 4 * GRID + 1
C_ALL = C_DIR + D

ROUNDS = CHUNKS + 3
LOOP_FROM, LOOP_TRIPS = 3, 5


class Chunk:

    def __init__(self, k, n):
        self.k, self.n, self.parity = k, n, n % 2

    def __sub__(self, m):
        return Chunk(self.k, self.n - m)

    def count(self, per_chunk, more=0):
        v = self.n * per_chunk + more
        return v if self.k is None else self.k * (2 * per_chunk) + v

    def pairs(self, per_pair, more=0):
        v = (self.n // 2) * per_pair + more
        return v if self.k is None else self.k * per_pair + v


class Round(Chunk):
    def __init__(self, k, n):
        Chunk.__init__(self, k, n)
        self.lstm0 = n < CHUNKS or k is not None
        self.ffn0 = 1 <= n <= CHUNKS or k is not None
        self.lstm1 = 2 <= n <= CHUNKS + 1 or k is not None
        self.ffn1 = n >= 3
        self.prepare = n < CHUNKS - 1 or k is not None


def run_rounds(engine, body):
    for n in range(LOOP_FROM):
        body(Round(None, n))
    if LOOP_TRIPS:
        with engine.Fori(0, LOOP_TRIPS) as k:
            body(Round(k, LOOP_FROM))
            body(Round(k, LOOP_FROM + 1))
    for n in range(LOOP_FROM + 2 * LOOP_TRIPS, ROUNDS):
        body(Round(None, n))


def build(nc, io, out):
    with ExitStack() as ctx:
        def sb(name, shape, dt=F32):
            return ctx.enter_context(nc.sbuf_tensor(name, shape, dt))

        def ps(name, shape):
            return ctx.enter_context(nc.psum_tensor(name, shape, F32))

        def sem(name):
            return ctx.enter_context(nc.semaphore(name))

        wx = [sb(f"wx{l}", [D, 4 * D]) for l in range(2)]
        wh = [sb(f"wh{l}", [D, 4 * D]) for l in range(2)]
        bias3 = sb("bias3", [3, 9 * D])
        part1 = sb("part1", [3, 9 * D], BF16)
        part2 = sb("part2", [3, 9 * D], BF16)
        part3 = sb("part3", [3, 9 * D], BF16)
        rest = sb("rest", [3, 9 * D])
        pick = sb("pick", [3, 9 * D])
        biasb = sb("biasb", [3, 9 * D], BF16)
        ones3 = sb("ones3", [3, TOK], BF16)
        ident = sb("ident", [128, 128])
        cond = sb("cond", [B, D])
        raw = sb("raw", [NT, D])
        sig_raw = sb("sig_raw", [D, NT])
        sig_a = sb("sig_a", [D, NT])
        sig_q = sb("sig_q", [D, NT])
        sig_t = sb("sig_t", [D, NT])
        csum = sb("csum", [D, 2, NC])
        cneg = sb("cneg", [D, NC])
        score_w = sb("score_w", [D, NC + NT])
        comp_w1 = sb("comp_w1", [D, CH])
        comp_b1 = sb("comp_b1", [CH, 1])
        comp_w2 = sb("comp_w2", [CH + 1, 2])
        temp = sb("temp", [128, 1])
        half_inv_temp = sb("half_inv_temp", [128, 1])
        knots = sb("knots", [128, KNOTS])
        slopes = sb("slopes", [128, KNOTS])
        kpos = sb("kpos", [128, KNOTS])
        rank = sb("rank", [128, NC])
        scale2 = sb("scale2", [128, 1])
        gamma = sb("gamma", [128, D])
        beta = sb("beta", [128, D])
        table = sb("table", [NT, C_ALL])
        win2 = sb("win2", [D, 2 * M])
        bin2 = sb("bin2", [2 * M, 1])
        kw1 = sb("kw1", [2 * M, HALF])
        kb1 = sb("kb1", [2 * M, HALF])
        kb1n = sb("kb1n", [2 * M, HALF])
        kw2 = sb("kw2", [2 * M, HALF])
        kb2 = sb("kb2", [M, 1])
        wout2 = sb("wout2", [2 * M, D])
        v_out = sb("v_out", [2 * M, HALF, D])
        bout = sb("bout", [1, D])
        crow = sb("crow", [1, D])
        table_load = sb("table_load", [128, 1])
        minus_half = sb("minus_half", [128, 1])

        x_tok = [sb(f"x_tok{p}", [TOK, D]) for p in range(2)]
        x_t = [sb(f"x_t{p}", [D, TOK]) for p in range(2)]
        x_beta = [sb(f"x_beta{p}", [TOK, D]) for p in range(2)]
        h = [[sb(f"h{l}_{p}", [D, TOK]) for p in range(2)] for l in range(2)]
        gates = [sb(f"gates{l}", [D, 5 * B]) for l in range(2)]
        mixed = [sb(f"mixed{l}", [D, 2 * B]) for l in range(2)]
        cell_tanh = [sb(f"cell_tanh{l}", [D, B]) for l in range(2)]
        tanhs = sb("tanhs", [TOK, NC + NT])
        sigm = sb("sigm", [TOK, NC + NT])
        picked = sb("picked", [TOK, TPC])
        away = sb("away", [TOK, NC * KNOTS])
        seg = sb("seg", [TOK, NC * KNOTS])
        gate_v = sb("gate_v", [TOK, NC])
        gate_m = sb("gate_m", [TOK, 1])
        ranks = sb("ranks", [TOK, NC])
        rank_m = sb("rank_m", [TOK, 1])
        in_cluster = sb("in_cluster", [TOK, NC])
        in_local = sb("in_local", [TOK, TPC])
        sel = sb("sel", [TOK, NT])
        one_hot = sb("one_hot", [TOK, 128])
        one_hot_t = sb("one_hot_t", [NT, TOK])
        spline = sb("spline", [TOK, C_DIR])
        gelu = sb("gelu", [CH + 1, TOK])
        comp = sb("comp", [TOK, 2])
        hidden = sb("hidden", [TOK, GRID])
        hidden2 = sb("hidden2", [TOK, GRID])
        hidden3 = sb("hidden3", [TOK, GRID])
        mag = sb("mag", [TOK, 1])
        mag2 = sb("mag2", [TOK, 1])
        h_tok = sb("h_tok", [TOK, D])
        y2 = sb("y2", [TOK, D])
        stats = sb("stats", [TOK, 6])
        mean_var = sb("mean_var", [TOK, 2])
        var_eps = sb("var_eps", [TOK, 1])
        rstd = sb("rstd", [TOK, 1])
        z = sb("z", [TOK, D])
        zg = sb("zg", [TOK, D])
        x1_tok = [sb(f"x1_tok{p}", [TOK, D]) for p in range(2)]
        x1_t = [sb(f"x1_t{p}", [D, TOK]) for p in range(2)]
        s1 = sb("s1", [2 * M, TOK])
        relus = sb("relus", [2 * M, HALF, TOK])
        o_tok = [sb(f"o_tok{p}", [TOK, D]) for p in range(2)]

        pre = [[ps(f"pre{l}_{p}", [D, 4, STEPS, B]) for p in range(2)] for l in range(2)]
        ps_a = ps("ps_a", [128, 512])
        ps_b = ps("ps_b", [128, 512])
        ps_c = ps("ps_c", [128, 512])
        ps_d = ps("ps_d", [128, 512])
        score_ps, compress_ps = ps_a[:, 0:NC + NT], ps_a[0:CH, 128:128 + TOK]
        turn_ps = ps_b[:, 0:128]

        w_lstm0, w_lstm1, w_ffn0, w_ffn1 = sem("w_lstm0"), sem("w_lstm1"), sem("w_ffn0"), sem("w_ffn1")
        table_loaded = sem("table_loaded")
        w_bias, w_cond, w_table = sem("w_bias"), sem("w_cond"), sem("w_table")
        x_loaded = [sem(f"x_loaded{p}") for p in range(2)]
        out_stored = [sem(f"out_stored{p}") for p in range(2)]
        const_ready = sem("const_ready")
        pool_step = sem("pool_step")
        ident_ready = sem("ident_ready")
        turned0 = sem("turned0")
        set_dve = sem("set_dve")
        lstm_w_ready = [sem(f"lstm_w_ready{l}") for l in range(2)]
        start_ready = sem("start_ready")
        bias_ready = sem("bias_ready")
        ffn0_w_ready = sem("ffn0_w_ready")
        ffn1_w_ready = sem("ffn1_w_ready")
        crow_ps_ready, crow_ready, crow_moved = sem("crow_ps_ready"), sem("crow_ready"), sem("crow_moved")
        crow_split = sem("crow_split")
        pre_ready = [sem(f"pre_ready{l}") for l in range(2)]
        gates_ready = [sem(f"gates_ready{l}") for l in range(2)]
        mixed_ready = [sem(f"mixed_ready{l}") for l in range(2)]
        cell_ready = [sem(f"cell_ready{l}") for l in range(2)]
        tanh_ready = [sem(f"tanh_ready{l}") for l in range(2)]
        h_ready = [sem(f"h_ready{l}") for l in range(2)]
        xt_ps_ready, xt_ready, x_beta_ready = sem("xt_ps_ready"), sem("xt_ready"), sem("x_beta_ready")
        scores_ready, tanhs_ready = sem("scores_ready"), sem("tanhs_ready")
        gelu_ready = sem("gelu_ready")
        comp_ps_ready, comp_ready = sem("comp_ps_ready"), sem("comp_ready")
        route = sem("route")
        one_hot_ready, one_hot_ps_ready, one_hot_t_ready = sem("one_hot_ready"), sem("one_hot_ps_ready"), sem("one_hot_t_ready")
        gathered, spline_ready = sem("gathered"), sem("spline_ready")
        h_tok_ps_ready, h_tok_ready = sem("h_tok_ps_ready"), sem("h_tok_ready")
        mag_step = sem("mag_step")
        norm_step = sem("norm_step")
        rstd_ready = sem("rstd_ready")
        zg_ready, x1_ready = sem("zg_ready"), sem("x1_ready")
        x1t_ps_ready, x1t_ready = sem("x1t_ps_ready"), sem("x1t_ready")
        s1_ps_ready, s1_ready, relus_ready = sem("s1_ps_ready"), sem("s1_ready"), sem("relus_ready")
        ffn1_ps_ready, o_ready = sem("ffn1_ps_ready"), sem("o_ready")
        ROUTE = 23

        x_dram = io["x"].rearrange("b (c t) d -> c t b d", t=STEPS)
        out_dram = out.rearrange("b (c t) d -> c t b d", t=STEPS)

        def row(name):
            return io[name].rearrange("(a d) -> a d", a=1)

        def column(name):
            return io[name].rearrange("(d a) -> d a", a=1)

        block = ctx.enter_context(nc.Block())

        @block.sync
        def _(sp):
            sp.dma_start(x_tok[0][:, :], x_dram[0]).then_inc(x_loaded[0], 16)
            sp.dma_start(wx[0][:, :], io["L0_cond_Wx"]).then_inc(w_lstm0, 16)
            sp.dma_start(wh[0][:, :], io["L0_cond_Wh"]).then_inc(w_lstm0, 16)
            sp.dma_start(x_tok[1][:, :], x_dram[1]).then_inc(x_loaded[1], 16)
            sp.dma_start(raw[:, :], io["L0_ffn_signatures_raw"]).then_inc(w_ffn0, 16)
            sp.dma_start(comp_w1[:, :], io["L0_ffn_compress_w1"]).then_inc(w_ffn0, 16)
            sp.dma_start(comp_b1[:, :], column("L0_ffn_compress_b1")).then_inc(w_ffn0, 16)
            sp.dma_start(comp_w2[0:CH, :], io["L0_ffn_compress_w2"]).then_inc(w_ffn0, 16)
            sp.dma_start(comp_w2[CH:CH + 1, :], row("L0_ffn_compress_b2")).then_inc(w_ffn0, 16)
            sp.dma_start(knots[:, :], row("L0_ffn_knot_values").to_broadcast([128, KNOTS])).then_inc(w_ffn0, 16)
            sp.dma_start(temp[:, :], row("L0_ffn_temperature").to_broadcast([128, 1])).then_inc(w_ffn0, 16)
            sp.dma_start(scale2[:, :], row("L0_ffn_output_scale").to_broadcast([128, 1])).then_inc(w_ffn0, 16)
            sp.dma_start(gamma[:, :], row("L0_ffn_norm_gamma").to_broadcast([128, D])).then_inc(w_ffn0, 16)
            sp.dma_start(beta[:, :], row("L0_ffn_norm_beta").to_broadcast([128, D])).then_inc(w_ffn0, 16)
            sp.dma_start(table[:, C_W1:C_B1], io["L0_ffn_spline_w1"].rearrange("n i g -> n (i g)")).then_inc(w_table, 16)
            sp.dma_start(table[:, C_B1:C_W2], io["L0_ffn_spline_b1"]).then_inc(w_table, 16)
            sp.dma_start(table[:, C_W2:C_B2], io["L0_ffn_spline_w2"].rearrange("n g o -> n (g o)")).then_inc(w_table, 16)
            sp.dma_start(table[:, C_B2:C_DIR], io["L0_ffn_spline_b2"]).then_inc(w_table, 16)
            sp.dma_start(table[:, C_DIR:C_ALL], io["L0_ffn_directions"]).then_inc(w_table, 16)
            sp.dma_start(wx[1][:, :], io["L1_cond_Wx"]).then_inc(w_lstm1, 16)
            sp.dma_start(wh[1][:, :], io["L1_cond_Wh"]).then_inc(w_lstm1, 16)
            for half in range(2):
                at, cols = slice(M * half, M * half + M), slice(HALF * half, HALF * half + HALF)
                sp.dma_start(win2[:, at], io["L1_ffn_Win"]).then_inc(w_ffn1, 16)
                sp.dma_start(bin2[at, :], column("L1_ffn_bin_")).then_inc(w_ffn1, 16)
                sp.dma_start(kw1[at, :], io["L1_ffn_W1"][:, cols]).then_inc(w_ffn1, 16)
                sp.dma_start(kb1[at, :], io["L1_ffn_b1"][:, cols]).then_inc(w_ffn1, 16)
                sp.dma_start(kw2[at, :], io["L1_ffn_W2"][:, cols]).then_inc(w_ffn1, 16)
                sp.dma_start(wout2[at, :], io["L1_ffn_Wout"]).then_inc(w_ffn1, 16)
            sp.dma_start(kb2[:, :], column("L1_ffn_b2")).then_inc(w_ffn1, 16)
            sp.wait_ge(crow_ready, 1)
            for q in range(3):
                sp.dma_start(bias3[q:q + 1, 8 * D:9 * D], crow[:, :]).then_inc(crow_moved, 16)

            def body(r):
                p = r.parity
                if r.n < CHUNKS - 2 or r.k is not None:
                    sp.wait_ge(x_beta_ready, r.count(1, 1))
                    sp.wait_ge(xt_ps_ready, r.count(1, 1))
                    src = x_dram[r.n + 2] if r.k is None else x_dram[r.k * 2 + (r.n + 2)]
                    sp.dma_start(x_tok[p][:, :], src).then_inc(x_loaded[p], 16)
                if r.ffn1:
                    c = r - 3
                    sp.wait_ge(o_ready, c.count(1, 1))
                    dst = out_dram[c.n] if c.k is None else out_dram[c.k * 2 + c.n]
                    sp.dma_start(dst, o_tok[c.parity][:, :]).then_inc(out_stored[c.parity], 16)

            run_rounds(sp, body)
            for p in range(2):
                sp.wait_ge(out_stored[p], 16 * CHUNKS // 2)

        @block.gpsimd
        def _(pool):
            nc.gpsimd.memset(ident[:, :], 0.0).then_inc(pool_step, 1)
            pool.wait_ge(pool_step, 1)
            nc.gpsimd.affine_select(out=ident[:, :], in_=ident[:, :], compare_op=ALU.not_equal, fill=1.0, base=0,
                                    pattern=[[-1, 128]], channel_multiplier=1).then_inc(ident_ready, 1)
            for l in range(2):
                nc.gpsimd.memset(gates[l][:, 4 * B:5 * B], 0.0).then_inc(const_ready, 1)
            nc.gpsimd.memset(ones3[:, :], 1.0).then_inc(const_ready, 1)
            nc.gpsimd.memset(one_hot[:, :], 0.0).then_inc(const_ready, 1)
            nc.gpsimd.memset(minus_half[:, :], -0.5).then_inc(const_ready, 1)
            for k in range(KNOTS):
                nc.gpsimd.memset(kpos[:, k:k + 1], float(k)).then_inc(const_ready, 1)
                nc.gpsimd.memset(rank[:, k:k + 1], float(NC - k)).then_inc(const_ready, 1)
            pool.wait_ge(w_lstm1, 32)
            nc.gpsimd.tensor_scalar(wx[1][:, 0:3 * D], wx[1][:, 0:3 * D], 0.5, 1.0, ALU.mult, ALU.mult).then_inc(lstm_w_ready[1], 1)
            nc.gpsimd.tensor_scalar(wh[1][:, 0:3 * D], wh[1][:, 0:3 * D], 0.25, 1.0, ALU.mult, ALU.mult).then_inc(lstm_w_ready[1], 1)
            nc.gpsimd.tensor_scalar(wh[1][:, 3 * D:], wh[1][:, 3 * D:], 0.5, 1.0, ALU.mult, ALU.mult).then_inc(lstm_w_ready[1], 1)
            pool.wait_ge(w_ffn0, 160)

            def body(r):
                if r.lstm0:
                    p = r.parity
                    if r.k is None and r.n == 0:
                        pool.wait_ge(x_loaded[0], 16)
                    else:
                        pool.wait_ge(x_loaded[p], r.pairs(16, 16))
                    if not (r.k is None and r.n < 2):
                        pool.wait_ge(x1_ready, r.count(1, -1))
                    nc.gpsimd.tensor_tensor(x_beta[p][:, :], x_tok[p][:, :], beta[:, :], ALU.add).then_inc(x_beta_ready, 1)
                if r.ffn0:
                    c = r - 1
                    q = c.parity
                    pool.wait_ge(route, c.count(ROUTE, ROUTE))
                    if not (c.k is None and c.n == 0):
                        pool.wait_ge(one_hot_ps_ready, c.count(1))
                    nc.gpsimd.tensor_tensor(
                        one_hot[:, 0:NT].rearrange("p (c j) -> p c j", c=NC),
                        in_cluster[:, :].unsqueeze(2).to_broadcast([TOK, NC, TPC]),
                        in_local[:, :].unsqueeze(1).to_broadcast([TOK, NC, TPC]), ALU.mult).then_inc(one_hot_ready, 1)
                    pool.wait_ge(norm_step, c.count(4, 3))
                    nc.gpsimd.tensor_tensor(rstd[:, :], var_eps[:, :], minus_half[:, :], ALU.pow).then_inc(rstd_ready, 1)
                    pool.wait_ge(norm_step, c.count(4, 4))
                    nc.gpsimd.tensor_tensor(zg[:, :], z[:, :], gamma[:, :], ALU.mult).then_inc(zg_ready, 1)
                    pool.wait_ge(zg_ready, c.count(1, 1))
                    pool.wait_ge(x_beta_ready, c.count(1, 1))
                    if not (c.k is None and c.n < 2):
                        pool.wait_ge(o_ready, c.count(1, -1))
                    nc.gpsimd.tensor_tensor(x1_tok[q][:, :], zg[:, :], x_beta[q][:, :], ALU.add).then_inc(x1_ready, 1)

            run_rounds(pool, body)

        @block.tensor
        def _(pe):
            pe.wait_ge(ident_ready, 1)
            pe.wait_ge(x_loaded[0], 16)
            pe.transpose(turn_ps, x_tok[0][:, :], ident[:, :]).then_inc(xt_ps_ready, 1)
            pe.wait_ge(w_cond, 16)
            pe.transpose(ps_c[:, 0:B], cond[:, :], ident[0:B, 0:B]).then_inc(turned0, 1)
            pe.wait_ge(w_ffn0, 160)
            pe.transpose(ps_d[:, 0:NT], raw[:, :], ident[0:NT, 0:NT]).then_inc(turned0, 1)

            def bias_part(l, p):
                for q, g in enumerate(GATE):
                    pe.matmul(pre[l][p][:, q].rearrange("d s b -> d (s b)"), biasb[:, (4 * l + g) * D:(4 * l + g + 1) * D],
                              ones3[:, :], start=(q == 0), stop=False, skip_group_check=True)

            def x_part(l, p, src, q, s0, s1_):
                g = GATE[q]
                pe.matmul(pre[l][p][:, q, s0:s1_].rearrange("d s b -> d (s b)"), wx[l][:, g * D:(g + 1) * D],
                          src[:, s0 * B:s1_ * B], start=False, stop=False, skip_group_check=True)

            def h_part(l, c, s):
                p = c.parity
                if c.k is None and c.n == 0 and s == 0:
                    pe.wait_ge(start_ready, 2)
                else:
                    pe.wait_ge(h_ready[l], c.count(STEPS, s))
                prev = h[l][p][:, (s - 1) * B:s * B] if s else h[l][1 - p][:, TOK - B:TOK]
                for q, g in enumerate(GATE):
                    mm = pe.matmul(pre[l][p][:, q, s], wh[l][:, g * D:(g + 1) * D], prev,
                                   start=False, stop=True, skip_group_check=True)
                mm.then_inc(pre_ready[l], 1)

            pe.wait_ge(bias_ready, 1)
            pe.wait_ge(const_ready, 5 + 2 * KNOTS)
            pe.wait_ge(lstm_w_ready[0], 3)
            pe.wait_ge(xt_ready, 1)
            bias_part(0, 0)
            for q in range(4):
                x_part(0, 0, x_t[0], q, 0, STEPS)
            pe.wait_ge(ffn1_w_ready, 1)
            pe.matmul(ps_d[0:1, 128:128 + D], kb2[:, :], wout2[0:M, :], start=True, stop=False)
            pe.matmul(ps_d[0:1, 128:128 + D], ident[0:1, 0:1], bout[:, :], start=False, stop=False)
            for j in range(HALF):
                mm = pe.matmul(ps_d[0:1, 128:128 + D], kb1[:, j:j + 1], v_out[:, j, :], start=False, stop=(j == HALF - 1))
            mm.then_inc(crow_ps_ready, 1)

            def body(r):
                p = r.parity
                c0, c1 = r - 1, r - 3
                first = r.k is None
                for s in range(STEPS):
                    if r.lstm0:
                        h_part(0, r, s)
                    if s == 0 and r.ffn0:
                        if first and r.n == 1:
                            pe.wait_ge(ffn0_w_ready, 3)
                        pe.wait_ge(h_ready[0], c0.count(STEPS, STEPS))
                        if not (first and r.n == 1):
                            pe.wait_ge(tanhs_ready, c0.count(1))
                            pe.wait_ge(gelu_ready, c0.count(1))
                        hs = h[0][c0.parity]
                        pe.matmul(score_ps, hs[:, :], score_w[:, :], start=True, stop=True)
                        pe.matmul(compress_ps, comp_w1[:, :], hs[:, :], start=True, stop=True).then_inc(scores_ready, 1)
                    if r.lstm1 and s == 0:
                        pe.wait_ge(lstm_w_ready[1], 3)
                        pe.wait_ge(x1t_ready, (r - 2).count(1, 1))
                        bias_part(1, p)
                        for q in range(4):
                            x_part(1, p, x1_t[p], q, 0, 4)
                    if r.lstm1 and s in (1, 2):
                        pe.wait_ge(gates_ready[1], (r - 2).count(STEPS, s))
                        for q in (2 * s - 2, 2 * s - 1):
                            x_part(1, p, x1_t[p], q, 4, STEPS)
                    if r.lstm1:
                        h_part(1, r - 2, s)
                    if s == 0 and r.ffn1:
                        if r.n == 3:
                            pe.wait_ge(crow_split, 1)
                        pe.wait_ge(h_ready[1], c1.count(STEPS, STEPS))
                        if not (first and r.n == 3):
                            pe.wait_ge(o_ready, c1.count(1))
                        pe.matmul(ps_d[:, 0:TOK], win2[:, :], h[1][c1.parity][:, :], start=True, stop=True).then_inc(s1_ps_ready, 1)
                    if s == 1 and r.prepare:
                        pe.wait_ge(x_loaded[1 - p], (r - 0).pairs(16, 16) if p == 0 else (r - 0).pairs(16, 32))
                        if r.n >= 2:
                            pe.wait_ge(x1t_ready, r.count(1, -1))
                        elif r.n == 0:
                            pe.wait_ge(xt_ready, 1)
                        pe.transpose(turn_ps, x_tok[1 - p][:, :], ident[:, :]).then_inc(xt_ps_ready, 1)
                    if s == 2 and r.ffn0:
                        if r.prepare:
                            pe.wait_ge(xt_ready, r.count(1, 2))
                        pe.transpose(turn_ps, h[0][c0.parity][:, :], ident[:, :]).then_inc(h_tok_ps_ready, 1)
                    if s == 3 and r.ffn0:
                        pe.wait_ge(h_tok_ready, c0.count(1, 1))
                        pe.wait_ge(gelu_ready, c0.count(1, 1))
                        pe.matmul(ps_b[:, 0:2], gelu[:, :], comp_w2[:, :], start=True, stop=True).then_inc(comp_ps_ready, 1)
                    if s == 2 and r.prepare:
                        bias_part(0, 1 - p)
                    if s in (3, 4, 5, 6) and r.prepare:
                        if s == 3:
                            pe.wait_ge(xt_ready, r.count(1, 2))
                        x_part(0, 1 - p, x_t[1 - p], s - 3, 0, STEPS)
                    if s in (3, 4, 5, 6) and r.ffn1:
                        if s == 3:
                            pe.wait_ge(s1_ready, c1.count(1, 1))
                            pe.matmul(ps_d[:, 0:D], ones3[:, :], biasb[:, 8 * D:9 * D], start=True, stop=False)
                        for j in (2 * s - 6, 2 * s - 5):
                            pe.wait_ge(relus_ready, c1.count(HALF, j + 1))
                            mm = pe.matmul(ps_d[:, 0:D], relus[:, j, :], v_out[:, j, :], start=False, stop=(j == HALF - 1))
                        if s == 6:
                            mm.then_inc(ffn1_ps_ready, 1)
                    if s == 4 and r.ffn0:
                        pe.wait_ge(comp_ready, c0.count(1, 1))
                        pe.wait_ge(one_hot_ready, c0.count(1, 1))
                        pe.transpose(turn_ps, one_hot[:, :], ident[:, :]).then_inc(one_hot_ps_ready, 1)
                    if s == 5 and r.ffn0:
                        if first and r.n == 1:
                            pe.wait_ge(w_table, 80)
                        pe.wait_ge(one_hot_t_ready, c0.count(1, 1))
                        pe.matmul(ps_c[:, 0:C_ALL], one_hot_t[:, :], table[:, :], start=True, stop=True).then_inc(gathered, 1)
                    if s == 7 and r.ffn0:
                        pe.wait_ge(x1_ready, c0.count(1, 1))
                        pe.transpose(turn_ps, x1_tok[c0.parity][:, :], ident[:, :]).then_inc(x1t_ps_ready, 1)

            run_rounds(pe, body)

        @block.scalar
        def _(act):
            act.dma_start(cond[:, :], io["cond_1024"]).then_inc(w_cond, 16)
            for q in range(3):
                act.dma_start(bias3[q:q + 1, 0:4 * D], row("L0_cond_b")).then_inc(w_bias, 16)
                act.dma_start(bias3[q:q + 1, 4 * D:8 * D], row("L1_cond_b")).then_inc(w_bias, 16)
            act.dma_start(bout[:, :], row("L1_ffn_bout")).then_inc(w_bias, 16)
            act.wait_ge(const_ready, 5 + 2 * KNOTS)
            nc.scalar.activation(table_load[:, :], minus_half[:, :], ACT.Gelu).then_inc(table_loaded, 1)
            act.wait_ge(xt_ps_ready, 1)
            nc.scalar.activation(x_t[0][:, :], turn_ps, ACT.Identity).then_inc(xt_ready, 1)
            act.wait_ge(crow_ps_ready, 1)
            nc.scalar.activation(crow[:, :], ps_d[0:1, 128:128 + D], ACT.Identity).then_inc(crow_ready, 1)

            def gate_tanh(l, c, s):
                act.wait_ge(pre_ready[l], c.count(STEPS, s + 1))
                nc.scalar.activation(gates[l][:, 0:4 * B].rearrange("d (g b) -> d g b", g=4),
                                     pre[l][c.parity][:, :, s], ACT.Tanh).then_inc(gates_ready[l], 1)

            def cell_tanh_(l, c, s):
                act.wait_ge(cell_ready[l], c.count(STEPS, s + 1))
                nc.scalar.activation(cell_tanh[l][:, :], gates[l][:, 4 * B:5 * B], ACT.Tanh, scale=0.5).then_inc(tanh_ready[l], 1)

            def body(r):
                p = r.parity
                c0, c1 = r - 1, r - 3
                for s in range(STEPS):
                    if r.lstm0:
                        gate_tanh(0, r, s)
                    if s == 1 and r.ffn0:
                        if not (r.k is None and r.n == 1):
                            act.wait_ge(comp_ps_ready, c0.count(1))
                        nc.scalar.activation(gelu[0:CH, :], compress_ps, ACT.Gelu, bias=comp_b1[:, :]).then_inc(gelu_ready, 1)
                    if s == 5 and r.ffn0:
                        act.wait_ge(one_hot_ps_ready, c0.count(1, 1))
                        nc.scalar.activation(one_hot_t[:, :], ps_b[0:NT, 0:TOK], ACT.Identity).then_inc(one_hot_t_ready, 1)
                    if r.lstm0:
                        cell_tanh_(0, r, s)
                    if s == 0 and r.ffn0:
                        act.wait_ge(scores_ready, c0.count(1, 1))
                        nc.scalar.activation(tanhs[:, :], score_ps, ACT.Tanh, scale=half_inv_temp[:, :]).then_inc(tanhs_ready, 1)
                    if r.lstm1:
                        gate_tanh(1, r - 2, s)
                    if s == 0 and r.ffn1:
                        act.wait_ge(s1_ps_ready, c1.count(1, 1))
                        if r.n == 3:
                            act.wait_ge(ffn1_w_ready, 1)
                        nc.scalar.activation(s1[:, :], ps_d[:, 0:TOK], ACT.Identity, bias=bin2[:, :]).then_inc(s1_ready, 1)
                    if s == 1 and r.prepare:
                        act.wait_ge(xt_ps_ready, r.count(1, 2))
                        nc.scalar.activation(x_t[1 - p][:, :], turn_ps, ACT.Identity).then_inc(xt_ready, 1)
                    if s == 2 and r.ffn0:
                        act.wait_ge(h_tok_ps_ready, c0.count(1, 1))
                        nc.scalar.activation(h_tok[:, :], turn_ps, ACT.Identity).then_inc(h_tok_ready, 1)
                    if s == 3 and r.ffn0:
                        act.wait_ge(comp_ps_ready, c0.count(1, 1))
                        nc.scalar.activation(comp[:, :], ps_b[:, 0:2], ACT.Tanh).then_inc(comp_ready, 1)
                    if s == 5 and r.ffn0:
                        act.wait_ge(gathered, c0.count(1, 1))
                        nc.scalar.activation(spline[:, :], ps_c[:, 0:C_DIR], ACT.Identity).then_inc(spline_ready, 1)
                    if r.lstm1:
                        cell_tanh_(1, r - 2, s)
                    if s == 7 and r.ffn0:
                        act.wait_ge(x1t_ps_ready, c0.count(1, 1))
                        nc.scalar.activation(x1_t[c0.parity][:, :], turn_ps, ACT.Identity).then_inc(x1t_ready, 1)

            run_rounds(act, body)

        @block.vector
        def _(dve):
            dve.wait_ge(w_bias, 112)
            nc.vector.tensor_scalar(bias3[:, 0:3 * D], bias3[:, 0:3 * D], 0.5, None, ALU.mult).then_inc(set_dve, 1)
            nc.vector.tensor_scalar(bias3[:, 4 * D:7 * D], bias3[:, 4 * D:7 * D], 0.5, None, ALU.mult).then_inc(set_dve, 1)
            dve.wait_ge(set_dve, 2)

            steps = [2]

            def step(ins):
                steps[0] += 1
                ins.then_inc(set_dve, 1)
                dve.wait_ge(set_dve, steps[0])

            def split(c0_, c1_):
                w = slice(c0_, c1_)
                step(nc.vector.tensor_copy(part1[:, w], bias3[:, w]))
                step(nc.vector.tensor_tensor(rest[:, w], bias3[:, w], part1[:, w], ALU.subtract))
                step(nc.vector.tensor_copy(part2[:, w], rest[:, w]))
                step(nc.vector.tensor_tensor(rest[:, w], rest[:, w], part2[:, w], ALU.subtract))
                step(nc.vector.tensor_copy(part3[:, w], rest[:, w]))
                step(nc.vector.tensor_scalar(pick[:, w], part1[:, w], ident[0:3, 0:1], None, ALU.mult))
                step(nc.vector.scalar_tensor_tensor(out=pick[:, w], in0=part2[:, w], scalar=ident[0:3, 1:2], in1=pick[:, w],
                                                    op0=ALU.mult, op1=ALU.add))
                return nc.vector.scalar_tensor_tensor(out=biasb[:, w], in0=part3[:, w], scalar=ident[0:3, 2:3], in1=pick[:, w],
                                                      op0=ALU.mult, op1=ALU.add)

            dve.wait_ge(ident_ready, 1)
            split(0, 8 * D).then_inc(bias_ready, 1)
            dve.wait_ge(w_lstm0, 32)
            nc.vector.tensor_scalar(wx[0][:, 0:3 * D], wx[0][:, 0:3 * D], 0.5, None, ALU.mult).then_inc(lstm_w_ready[0], 1)
            nc.vector.tensor_scalar(wh[0][:, 0:3 * D], wh[0][:, 0:3 * D], 0.25, None, ALU.mult).then_inc(lstm_w_ready[0], 1)
            nc.vector.tensor_scalar(wh[0][:, 3 * D:], wh[0][:, 3 * D:], 0.5, None, ALU.mult).then_inc(lstm_w_ready[0], 1)
            dve.wait_ge(turned0, 1)
            for l in range(2):
                nc.vector.tensor_scalar(h[l][1][:, TOK - B:TOK], ps_c[:, 0:B], 2.0, None, ALU.mult).then_inc(start_ready, 1)
            dve.wait_ge(turned0, 2)
            step(nc.vector.tensor_copy(sig_raw[:, :], ps_d[:, 0:NT]))
            step(nc.vector.tensor_scalar(sig_a[:, :], sig_raw[:, :], -0.3, -1.0, ALU.is_lt, ALU.mult))
            step(nc.vector.scalar_tensor_tensor(out=sig_q[:, :], in0=sig_raw[:, :], scalar=0.3, in1=sig_a[:, :],
                                                op0=ALU.is_gt, op1=ALU.add))
            step(nc.vector.tensor_tensor(sig_a[:, :], sig_q[:, :], sig_raw[:, :], ALU.subtract))
            step(nc.vector.tensor_tensor(sig_t[:, :], sig_raw[:, :], sig_a[:, :], ALU.add))
            tiles = sig_t[:, :].rearrange("d (c j) -> d c j", c=NC)
            step(nc.vector.tensor_tensor(csum[:, 1], tiles[:, :, 0], tiles[:, :, 1], ALU.add))
            for j in range(2, TPC):
                step(nc.vector.tensor_tensor(csum[:, j % 2], csum[:, (j + 1) % 2], tiles[:, :, j], ALU.add))
            total = csum[:, (TPC - 1) % 2]
            step(nc.vector.tensor_scalar(cneg[:, :], total, 0.0, 0.5, ALU.is_lt, ALU.mult))
            nc.vector.tensor_scalar(score_w[:, NC:], sig_t[:, :], 0.5, None, ALU.mult)
            step(nc.vector.tensor_scalar(csum[:, TPC % 2], total, 0.0, 0.5, ALU.is_gt, ALU.mult))
            nc.vector.tensor_tensor(score_w[:, 0:NC], csum[:, TPC % 2], cneg[:, :], ALU.subtract).then_inc(ffn0_w_ready, 1)
            nc.vector.tensor_scalar(comp_w1[:, :], comp_w1[:, :], 0.5, None, ALU.mult)
            nc.vector.tensor_scalar(scale2[:, :], scale2[:, :], 2.0, None, ALU.mult)
            nc.vector.memset(slopes[:, KNOTS - 1:KNOTS], 0.0)
            nc.vector.memset(gelu[CH:CH + 1, :], 1.0)
            nc.vector.tensor_tensor(slopes[:, 0:KNOTS - 1], knots[:, 1:KNOTS], knots[:, 0:KNOTS - 1], ALU.subtract).then_inc(ffn0_w_ready, 1)
            step(nc.vector.tensor_scalar(temp[:, :], temp[:, :], 1e-6, None, ALU.add))
            step(nc.vector.reciprocal(half_inv_temp[:, :], temp[:, :]))
            nc.vector.tensor_scalar(half_inv_temp[:, :], half_inv_temp[:, :], 0.5, None, ALU.mult).then_inc(ffn0_w_ready, 1)
            dve.wait_ge(w_ffn1, 208)
            nc.vector.tensor_scalar(win2[:, :], win2[:, :], 0.5, None, ALU.mult)
            nc.vector.tensor_scalar(kb1n[:, :], kb1[:, :], -1.0, None, ALU.mult)
            for j in range(HALF):
                last = nc.vector.tensor_scalar(v_out[:, j, :], wout2[:, :], kw2[:, j:j + 1], None, ALU.mult)
            last.then_inc(ffn1_w_ready, 1)
            dve.wait_ge(const_ready, 5 + 2 * KNOTS)

            def lstm_cell(l, c, s):
                n = c.count(STEPS, s + 1)
                dve.wait_ge(gates_ready[l], n)
                nc.vector.scalar_tensor_tensor(out=mixed[l][:, :], in0=gates[l][:, B:3 * B], scalar=1.0, in1=gates[l][:, 3 * B:5 * B],
                                               op0=ALU.add, op1=ALU.mult).then_inc(mixed_ready[l], 1)
                dve.wait_ge(mixed_ready[l], n)
                nc.vector.scalar_tensor_tensor(out=gates[l][:, 4 * B:5 * B], in0=mixed[l][:, B:2 * B], scalar=0.5,
                                               in1=mixed[l][:, 0:B], op0=ALU.mult, op1=ALU.add).then_inc(cell_ready[l], 1)

            def lstm_h(l, c, s):
                dve.wait_ge(tanh_ready[l], c.count(STEPS, s + 1))
                nc.vector.scalar_tensor_tensor(out=h[l][c.parity][:, s * B:(s + 1) * B], in0=gates[l][:, 0:B], scalar=1.0,
                                               in1=cell_tanh[l][:, :], op0=ALU.add, op1=ALU.mult).then_inc(h_ready[l], 1)

            def calibrate(src, c, n):
                def wide(ap):
                    return ap.unsqueeze(2).to_broadcast([TOK, NC, KNOTS])

                def knotwise(ap):
                    return ap[:, :].unsqueeze(1).to_broadcast([TOK, NC, KNOTS])
                a3 = away[:, :].rearrange("p (c k) -> p c k", c=NC)
                s3 = seg[:, :].rearrange("p (c k) -> p c k", c=NC)
                nc.vector.scalar_tensor_tensor(out=a3, in0=wide(src), scalar=float(KNOTS - 1), in1=knotwise(kpos),
                                               op0=ALU.mult, op1=ALU.subtract).then_inc(route, 1)
                dve.wait_ge(route, c.count(ROUTE, n + 1))
                nc.vector.tensor_tensor(s3, a3, knotwise(slopes), ALU.mult).then_inc(route, 1)
                dve.wait_ge(route, c.count(ROUTE, n + 2))
                nc.vector.tensor_tensor(s3, s3, knotwise(knots), ALU.add).then_inc(route, 1)
                dve.wait_ge(route, c.count(ROUTE, n + 3))
                nc.vector.scalar_tensor_tensor(out=s3, in0=a3, scalar=1.0, in1=s3, op0=ALU.is_lt, op1=ALU.mult).then_inc(route, 1)
                dve.wait_ge(route, c.count(ROUTE, n + 4))
                nc.vector.scalar_tensor_tensor(out=s3, in0=a3, scalar=0.0, in1=s3, op0=ALU.is_ge, op1=ALU.mult).then_inc(route, 1)
                dve.wait_ge(route, c.count(ROUTE, n + 5))
                nc.vector.tensor_reduce(gate_v[:, :], s3, AX_X, ALU.add).then_inc(route, 1)

            def first_of_largest(dst, c, n):
                dve.wait_ge(route, c.count(ROUTE, n))
                nc.vector.tensor_reduce(gate_m[:, :], gate_v[:, :], AX_X, ALU.max).then_inc(route, 1)
                dve.wait_ge(route, c.count(ROUTE, n + 1))
                nc.vector.scalar_tensor_tensor(out=ranks[:, :], in0=gate_v[:, :], scalar=gate_m[:, :], in1=rank[:, :],
                                               op0=ALU.is_equal, op1=ALU.mult).then_inc(route, 1)
                dve.wait_ge(route, c.count(ROUTE, n + 2))
                nc.vector.tensor_reduce(rank_m[:, :], ranks[:, :], AX_X, ALU.max).then_inc(route, 1)
                dve.wait_ge(route, c.count(ROUTE, n + 3))
                nc.vector.tensor_scalar(dst[:, :], rank[:, :], rank_m[:, :], None, ALU.is_equal).then_inc(route, 1)

            def body(r):
                c0, c1 = r - 1, r - 3
                for s in range(STEPS):
                    if r.lstm0:
                        lstm_cell(0, r, s)
                    if s == 1 and r.ffn0:
                        dve.wait_ge(tanhs_ready, c0.count(1, 1))
                        if not (r.k is None and r.n == 1):
                            dve.wait_ge(one_hot_ready, c0.count(1))
                        nc.vector.tensor_scalar(sigm[:, :], tanhs[:, :], 0.5, 0.5, ALU.mult, ALU.add).then_inc(route, 1)
                        dve.wait_ge(route, c0.count(ROUTE, 1))
                        calibrate(sigm[:, 0:NC], c0, 1)
                    if s == 3 and r.ffn0:
                        calibrate(picked[:, :], c0, 13)
                    if s == 5 and r.ffn0:
                        pass
                    if r.lstm0:
                        lstm_h(0, r, s)
                    if s == 1 and r.ffn0:
                        first_of_largest(in_cluster, c0, 7)
                    if s == 3 and r.ffn0:
                        first_of_largest(in_local, c0, 19)
                    if r.lstm1:
                        lstm_cell(1, r - 2, s)
                    if s == 2 and r.ffn0:
                        dve.wait_ge(route, c0.count(ROUTE, 11))
                        nc.vector.tensor_tensor(sel[:, :].rearrange("p (j c) -> p c j", j=TPC),
                                                sigm[:, NC:].rearrange("p (c j) -> p c j", c=NC),
                                                in_cluster[:, :].unsqueeze(2).to_broadcast([TOK, NC, TPC]),
                                                ALU.mult).then_inc(route, 1)
                        dve.wait_ge(route, c0.count(ROUTE, 12))
                        nc.vector.tensor_reduce(picked[:, :], sel[:, :].rearrange("p (j c) -> p j c", j=TPC), AX_X,
                                                ALU.add).then_inc(route, 1)
                        dve.wait_ge(route, c0.count(ROUTE, 13))
                    if s == 6 and r.ffn0:
                        dve.wait_ge(spline_ready, c0.count(1, 1))
                        dve.wait_ge(comp_ready, c0.count(1, 1))
                        nc.vector.scalar_tensor_tensor(out=hidden[:, :], in0=spline[:, 0:GRID], scalar=comp[:, 0:1],
                                                       in1=spline[:, C_B1:C_W2], op0=ALU.mult, op1=ALU.add).then_inc(mag_step, 1)
                        dve.wait_ge(mag_step, c0.count(5, 1))
                        nc.vector.scalar_tensor_tensor(out=hidden2[:, :], in0=spline[:, GRID:2 * GRID], scalar=comp[:, 1:2],
                                                       in1=hidden[:, :], op0=ALU.mult, op1=ALU.add).then_inc(mag_step, 1)
                        dve.wait_ge(mag_step, c0.count(5, 2))
                        nc.vector.scalar_tensor_tensor(out=hidden3[:, :], in0=hidden2[:, :], scalar=0.0, in1=spline[:, C_W2:C_B2],
                                                       op0=ALU.max, op1=ALU.mult, accum_out=mag[:, :]).then_inc(mag_step, 1)
                        dve.wait_ge(mag_step, c0.count(5, 3))
                        nc.vector.tensor_scalar(mag2[:, :], mag[:, :], spline[:, C_B2:C_DIR], scale2[:, :],
                                                ALU.add, ALU.mult).then_inc(mag_step, 1)
                        dve.wait_ge(mag_step, c0.count(5, 4))
                        dve.wait_ge(h_tok_ready, c0.count(1, 1))
                        nc.vector.scalar_tensor_tensor(out=y2[:, :], in0=ps_c[:, C_DIR:C_ALL], scalar=mag2[:, :], in1=h_tok[:, :],
                                                       op0=ALU.mult, op1=ALU.add).then_inc(mag_step, 1)
                        dve.wait_ge(mag_step, c0.count(5, 5))
                        nc.vector.bn_stats(stats[:, :], y2[:, :]).then_inc(norm_step, 1)
                        dve.wait_ge(norm_step, c0.count(4, 1))
                    if r.lstm1:
                        lstm_h(1, r - 2, s)
                    if s == 6 and r.ffn0:
                        nc.vector.bn_aggr(mean_var[:, :], stats[:, :]).then_inc(norm_step, 1)
                        dve.wait_ge(norm_step, c0.count(4, 2))
                        nc.vector.tensor_scalar(var_eps[:, :], mean_var[:, 1:2], 4.0 * EPS_LN, None, ALU.add).then_inc(norm_step, 1)
                    if s == 7 and r.ffn0:
                        dve.wait_ge(rstd_ready, c0.count(1, 1))
                        nc.vector.tensor_scalar(z[:, :], y2[:, :], mean_var[:, 0:1], rstd[:, :], ALU.subtract, ALU.mult).then_inc(norm_step, 1)
                    if s in (2, 3, 4, 5) and r.ffn1:
                        dve.wait_ge(s1_ready, c1.count(1, 1))
                        if s == 2 and not (r.k is None and r.n == 3):
                            dve.wait_ge(ffn1_ps_ready, c1.count(1))
                        for j in (2 * s - 4, 2 * s - 3):
                            nc.vector.tensor_scalar(relus[:, j, :], s1[:, :], kw1[:, j:j + 1], kb1n[:, j:j + 1],
                                                    ALU.mult, ALU.max).then_inc(relus_ready, 1)
                    if s == 7 and r.ffn1:
                        dve.wait_ge(ffn1_ps_ready, c1.count(1, 1))
                        if not (r.k is None and r.n < 5):
                            dve.wait_ge(out_stored[c1.parity], c1.pairs(16))
                        nc.vector.tensor_tensor(o_tok[c1.parity][:, :], ps_d[:, 0:D], x1_tok[c1.parity][:, :], ALU.add).then_inc(o_ready, 1)
                if r.k is None and r.n == 2:
                    dve.wait_ge(crow_moved, 48)
                    split(8 * D, 9 * D).then_inc(crow_split, 1)

            run_rounds(dve, body)


_INS = ['x', 'cond_1024', 'L0_cond_Wx', 'L0_cond_Wh', 'L0_cond_b', 'L0_ffn_signatures_raw', 'L0_ffn_knot_values',
        'L0_ffn_temperature', 'L0_ffn_compress_w1', 'L0_ffn_compress_b1', 'L0_ffn_compress_w2', 'L0_ffn_compress_b2',
        'L0_ffn_spline_w1', 'L0_ffn_spline_b1', 'L0_ffn_spline_w2', 'L0_ffn_spline_b2', 'L0_ffn_directions',
        'L0_ffn_norm_gamma', 'L0_ffn_norm_beta', 'L0_ffn_output_scale', 'L1_cond_Wx', 'L1_cond_Wh', 'L1_cond_b',
        'L1_ffn_Win', 'L1_ffn_bin_', 'L1_ffn_W1', 'L1_ffn_b1', 'L1_ffn_W2', 'L1_ffn_b2', 'L1_ffn_Wout', 'L1_ffn_bout']


def kernel(**inputs):
    import numpy as _np
    import concourse.bacc as _bacc
    from concourse import mybir as _mybir
    from concourse.bass_utils import run_bass_kernel_spmd as _run

    nc = _bacc.Bacc("TRN2", target_bir_lowering=False, num_devices=1)
    arrays, io = {}, {}
    for name in _INS:
        a = _np.ascontiguousarray(inputs[name])
        arrays[f"in_{name}"] = a
        io[name] = nc.dram_tensor(f"in_{name}", a.shape, _mybir.dt.from_np(a.dtype), kind="ExternalInput").ap()
    out = nc.dram_tensor("out_x", (B, T, D), _mybir.dt.float32, kind="ExternalOutput").ap()
    build(nc, io, out)
    r = _run(nc, [arrays], core_ids=[0])
    return r.results[0]["out_x"]
```

```python
from contextlib import ExitStack

import numpy as np

import concourse.bass as bass
from concourse import mybir

ALU = mybir.AluOpType
ACT = mybir.ActivationFunctionType
F32 = mybir.dt.float32
BF16 = mybir.dt.bfloat16
AX_X = mybir.AxisListType.X

B, T, D = 16, 128, 128
STEPS = 8
TOK = STEPS * B
CHUNKS = T // STEPS
NT, NC, TPC = 64, 8, 8
KNOTS = 8
CH = 32
GRID = 16
M, INNER = 64, 16
HALF = INNER // 2
GATE = [2, 0, 1, 3]
EPS_LN = 1e-5

C_W1, C_B1, C_W2, C_B2, C_DIR = 0, 2 * GRID, 3 * GRID, 4 * GRID, 4 * GRID + 1
C_ALL = C_DIR + D

ROUNDS = CHUNKS + 3
ROUTE_AT, INNER_AT, SPLINE_AT, AGGR_SLOT = 4, 7, (21, 22, 23, 24, 25, 26, 27, 29), 6
ONE_HOT_SLOT = 4
LOOP_FROM, LOOP_TRIPS = 3, 5


class Chunk:

    def __init__(self, k, n):
        self.k, self.n, self.parity = k, n, n % 2

    def __sub__(self, m):
        return Chunk(self.k, self.n - m)

    def count(self, per_chunk, more=0):
        v = self.n * per_chunk + more
        return v if self.k is None else self.k * (2 * per_chunk) + v

    def pairs(self, per_pair, more=0):
        v = (self.n // 2) * per_pair + more
        return v if self.k is None else self.k * per_pair + v


class Round(Chunk):
    def __init__(self, k, n):
        Chunk.__init__(self, k, n)
        self.lstm0 = n < CHUNKS or k is not None
        self.ffn0 = 1 <= n <= CHUNKS or k is not None
        self.lstm1 = 2 <= n <= CHUNKS + 1 or k is not None
        self.ffn1 = n >= 3
        self.prepare = n < CHUNKS - 1 or k is not None


def run_rounds(engine, body):
    for n in range(LOOP_FROM):
        body(Round(None, n))
    if LOOP_TRIPS:
        with engine.Fori(0, LOOP_TRIPS) as k:
            body(Round(k, LOOP_FROM))
            body(Round(k, LOOP_FROM + 1))
    for n in range(LOOP_FROM + 2 * LOOP_TRIPS, ROUNDS):
        body(Round(None, n))


def build(nc, io, out):
    with ExitStack() as ctx:
        def sb(name, shape, dt=F32):
            return ctx.enter_context(nc.sbuf_tensor(name, shape, dt))

        def ps(name, shape):
            return ctx.enter_context(nc.psum_tensor(name, shape, F32))

        def sem(name):
            return ctx.enter_context(nc.semaphore(name))

        wx = [sb(f"wx{l}", [D, 4 * D]) for l in range(2)]
        wh = [sb(f"wh{l}", [D, 4 * D]) for l in range(2)]
        whb = [sb(f"whb{l}", [D, 3, 4 * D], BF16) for l in range(2)]
        bias3 = sb("bias3", [3, 9 * D])
        part1 = sb("part1", [3, 9 * D], BF16)
        part2 = sb("part2", [3, 9 * D], BF16)
        part3 = sb("part3", [3, 9 * D], BF16)
        rest = sb("rest", [3, 9 * D])
        pick = sb("pick", [3, 9 * D])
        biasb = sb("biasb", [3, 9 * D], BF16)
        ones3 = sb("ones3", [3, TOK], BF16)
        ident = sb("ident", [128, 128])
        cond = sb("cond", [B, D])
        raw = sb("raw", [NT, D])
        sig_raw = sb("sig_raw", [D, NT])
        sig_a = sb("sig_a", [D, NT])
        sig_q = sb("sig_q", [D, NT])
        sig_t = sb("sig_t", [D, NT])
        csum = sb("csum", [D, 2, NC])
        cneg = sb("cneg", [D, NC])
        score_w = sb("score_w", [D, NC + NT])
        comp_w1 = sb("comp_w1", [D, CH])
        comp_b1 = sb("comp_b1", [CH, 1])
        comp_w2 = sb("comp_w2", [CH + 1, 2])
        temp = sb("temp", [128, 1])
        half_inv_temp = sb("half_inv_temp", [128, 1])
        knots = sb("knots", [128, KNOTS])
        slopes = sb("slopes", [128, KNOTS])
        kpos = sb("kpos", [128, KNOTS])
        rank = sb("rank", [128, NC])
        scale2 = sb("scale2", [128, 1])
        gamma = sb("gamma", [128, D])
        beta = sb("beta", [128, D])
        table = sb("table", [NT, C_ALL])
        win2 = sb("win2", [D, 2 * M])
        bin2 = sb("bin2", [2 * M, 1])
        kw1 = sb("kw1", [2 * M, HALF])
        kb1 = sb("kb1", [2 * M, HALF])
        kw2 = sb("kw2", [2 * M, HALF])
        kb2 = sb("kb2", [M, 1])
        wout2 = sb("wout2", [2 * M, D])
        bout = sb("bout", [1, D])
        crow = sb("crow", [1, D])
        table_load = sb("table_load", [128, 1])
        minus_half = sb("minus_half", [128, 1])

        x_tok = [sb(f"x_tok{p}", [TOK, D]) for p in range(2)]
        x_t = [sb(f"x_t{p}", [D, TOK]) for p in range(2)]
        x_beta = [sb(f"x_beta{p}", [TOK, D]) for p in range(2)]
        h = [[sb(f"h{l}_{p}", [D, TOK]) for p in range(2)] for l in range(2)]
        hb = [sb(f"hb{l}", [D, 3, B], BF16) for l in range(2)]
        h_rest = [sb(f"h_rest{l}", [D, B]) for l in range(2)]
        gates = [sb(f"gates{l}", [D, 5 * B]) for l in range(2)]
        mixed = [sb(f"mixed{l}", [D, 2 * B]) for l in range(2)]
        cell_tanh = [sb(f"cell_tanh{l}", [D, B]) for l in range(2)]
        tanhs = sb("tanhs", [TOK, NC + NT])
        sigm = sb("sigm", [TOK, NC + NT])
        picked = sb("picked", [TOK, TPC])
        away = sb("away", [TOK, NC * KNOTS])
        seg = sb("seg", [TOK, NC * KNOTS])
        gate_v = sb("gate_v", [TOK, NC])
        gate_m = sb("gate_m", [TOK, 1])
        ranks = sb("ranks", [TOK, NC])
        rank_m = sb("rank_m", [TOK, 1])
        in_cluster = sb("in_cluster", [TOK, NC])
        in_local = sb("in_local", [TOK, TPC])
        sel = sb("sel", [TOK, NT])
        one_hot = sb("one_hot", [TOK, 128])
        one_hot_t = sb("one_hot_t", [NT, TOK])
        spline = sb("spline", [TOK, C_DIR])
        gelu = sb("gelu", [CH + 1, TOK])
        comp = sb("comp", [TOK, 2])
        hidden = sb("hidden", [TOK, GRID])
        hidden2 = sb("hidden2", [TOK, GRID])
        hidden3 = sb("hidden3", [TOK, GRID])
        mag = sb("mag", [TOK, 1])
        mag2 = sb("mag2", [TOK, 1])
        h_tok = sb("h_tok", [TOK, D])
        y2 = sb("y2", [TOK, D])
        stats = sb("stats", [TOK, 6])
        mean_var = sb("mean_var", [TOK, 2])
        var_eps = sb("var_eps", [TOK, 1])
        rstd = sb("rstd", [TOK, 1])
        z = sb("z", [TOK, D])
        zg = sb("zg", [TOK, D])
        x1_tok = [sb(f"x1_tok{p}", [TOK, D]) for p in range(2)]
        x1_t = [sb(f"x1_t{p}", [D, TOK]) for p in range(2)]
        s1 = sb("s1", [2 * M, TOK])
        relus = sb("relus", [2 * M, HALF, TOK])
        inner = sb("inner", [2 * M, TOK])
        o_tok = [sb(f"o_tok{p}", [TOK, D]) for p in range(2)]

        pre = [[ps(f"pre{l}_{p}", [D, 4, STEPS, B]) for p in range(2)] for l in range(2)]
        ps_a = ps("ps_a", [128, 512])
        ps_b = ps("ps_b", [128, 512])
        ps_c = ps("ps_c", [128, 512])
        ps_d = ps("ps_d", [128, 512])
        score_ps, compress_ps = ps_a[:, 0:NC + NT], ps_a[0:CH, 128:128 + TOK]
        turn_ps = ps_b[:, 0:128]

        w_lstm0, w_lstm1, w_ffn0, w_ffn1 = sem("w_lstm0"), sem("w_lstm1"), sem("w_ffn0"), sem("w_ffn1")
        table_loaded = sem("table_loaded")
        w_bias, w_cond, w_table = sem("w_bias"), sem("w_cond"), sem("w_table")
        x_loaded = [sem(f"x_loaded{p}") for p in range(2)]
        out_stored = [sem(f"out_stored{p}") for p in range(2)]
        const_ready = sem("const_ready")
        pool_step = sem("pool_step")
        ident_ready = sem("ident_ready")
        turned0 = sem("turned0")
        set_dve = sem("set_dve")
        lstm_w_ready = [sem(f"lstm_w_ready{l}") for l in range(2)]
        start_ready = sem("start_ready")
        bias_ready = sem("bias_ready")
        ffn0_w_ready = sem("ffn0_w_ready")
        ffn1_w_ready = sem("ffn1_w_ready")
        crow_ps_ready, crow_ready, crow_moved = sem("crow_ps_ready"), sem("crow_ready"), sem("crow_moved")
        crow_split = sem("crow_split")
        pre_ready = [sem(f"pre_ready{l}") for l in range(2)]
        gates_ready = [sem(f"gates_ready{l}") for l in range(2)]
        mixed_ready = [sem(f"mixed_ready{l}") for l in range(2)]
        cell_ready = [sem(f"cell_ready{l}") for l in range(2)]
        tanh_ready = [sem(f"tanh_ready{l}") for l in range(2)]
        h_ready = [sem(f"h_ready{l}") for l in range(2)]
        part_ready = [[sem(f"part{q}_ready{l}") for q in range(3)] for l in range(2)]
        rest_ready = [sem(f"rest_ready{l}") for l in range(2)]
        xt_ps_ready, xt_ready, x_beta_ready = sem("xt_ps_ready"), sem("xt_ready"), sem("x_beta_ready")
        scores_ready, tanhs_ready = sem("scores_ready"), sem("tanhs_ready")
        gelu_ready = sem("gelu_ready")
        comp_ps_ready, comp_ready = sem("comp_ps_ready"), sem("comp_ready")
        route = sem("route")
        one_hot_ready, one_hot_ps_ready, one_hot_t_ready = sem("one_hot_ready"), sem("one_hot_ps_ready"), sem("one_hot_t_ready")
        gathered, spline_ready = sem("gathered"), sem("spline_ready")
        h_tok_ps_ready, h_tok_ready = sem("h_tok_ps_ready"), sem("h_tok_ready")
        mag_step = sem("mag_step")
        norm_step = sem("norm_step")
        rstd_ready = sem("rstd_ready")
        zg_ready, x1_ready = sem("zg_ready"), sem("x1_ready")
        x1t_ps_ready, x1t_ready = sem("x1t_ps_ready"), sem("x1t_ready")
        s1_ps_ready, s1_ready, relus_ready = sem("s1_ps_ready"), sem("s1_ready"), sem("relus_ready")
        inner_step = sem("inner_step")
        l1_split = sem("l1_split")
        ffn1_ps_ready, o_ready = sem("ffn1_ps_ready"), sem("o_ready")
        ROUTE = 23

        x_dram = io["x"].rearrange("b (c t) d -> c t b d", t=STEPS)
        out_dram = out.rearrange("b (c t) d -> c t b d", t=STEPS)

        def row(name):
            return io[name].rearrange("(a d) -> a d", a=1)

        def column(name):
            return io[name].rearrange("(d a) -> d a", a=1)

        block = ctx.enter_context(nc.Block())

        @block.sync
        def _(sp):
            sp.dma_start(x_tok[0][:, :], x_dram[0]).then_inc(x_loaded[0], 16)
            sp.dma_start(wx[0][:, :], io["L0_cond_Wx"]).then_inc(w_lstm0, 16)
            sp.dma_start(wh[0][:, :], io["L0_cond_Wh"]).then_inc(w_lstm0, 16)
            sp.dma_start(x_tok[1][:, :], x_dram[1]).then_inc(x_loaded[1], 16)
            sp.dma_start(raw[:, :], io["L0_ffn_signatures_raw"]).then_inc(w_ffn0, 16)
            sp.dma_start(comp_w1[:, :], io["L0_ffn_compress_w1"]).then_inc(w_ffn0, 16)
            sp.dma_start(comp_b1[:, :], column("L0_ffn_compress_b1")).then_inc(w_ffn0, 16)
            sp.dma_start(comp_w2[0:CH, :], io["L0_ffn_compress_w2"]).then_inc(w_ffn0, 16)
            sp.dma_start(comp_w2[CH:CH + 1, :], row("L0_ffn_compress_b2")).then_inc(w_ffn0, 16)
            sp.dma_start(knots[:, :], row("L0_ffn_knot_values").to_broadcast([128, KNOTS])).then_inc(w_ffn0, 16)
            sp.dma_start(temp[:, :], row("L0_ffn_temperature").to_broadcast([128, 1])).then_inc(w_ffn0, 16)
            sp.dma_start(scale2[:, :], row("L0_ffn_output_scale").to_broadcast([128, 1])).then_inc(w_ffn0, 16)
            sp.dma_start(gamma[:, :], row("L0_ffn_norm_gamma").to_broadcast([128, D])).then_inc(w_ffn0, 16)
            sp.dma_start(beta[:, :], row("L0_ffn_norm_beta").to_broadcast([128, D])).then_inc(w_ffn0, 16)
            sp.dma_start(table[:, C_W1:C_B1], io["L0_ffn_spline_w1"].rearrange("n i g -> n (i g)")).then_inc(w_table, 16)
            sp.dma_start(table[:, C_B1:C_W2], io["L0_ffn_spline_b1"]).then_inc(w_table, 16)
            sp.dma_start(table[:, C_W2:C_B2], io["L0_ffn_spline_w2"].rearrange("n g o -> n (g o)")).then_inc(w_table, 16)
            sp.dma_start(table[:, C_B2:C_DIR], io["L0_ffn_spline_b2"]).then_inc(w_table, 16)
            sp.dma_start(table[:, C_DIR:C_ALL], io["L0_ffn_directions"]).then_inc(w_table, 16)
            sp.dma_start(wx[1][:, :], io["L1_cond_Wx"]).then_inc(w_lstm1, 16)
            sp.dma_start(wh[1][:, :], io["L1_cond_Wh"]).then_inc(w_lstm1, 16)
            for half in range(2):
                at, cols = slice(M * half, M * half + M), slice(HALF * half, HALF * half + HALF)
                sp.dma_start(win2[:, at], io["L1_ffn_Win"]).then_inc(w_ffn1, 16)
                sp.dma_start(bin2[at, :], column("L1_ffn_bin_")).then_inc(w_ffn1, 16)
                sp.dma_start(kw1[at, :], io["L1_ffn_W1"][:, cols]).then_inc(w_ffn1, 16)
                sp.dma_start(kb1[at, :], io["L1_ffn_b1"][:, cols]).then_inc(w_ffn1, 16)
                sp.dma_start(kw2[at, :], io["L1_ffn_W2"][:, cols]).then_inc(w_ffn1, 16)
                sp.dma_start(wout2[at, :], io["L1_ffn_Wout"]).then_inc(w_ffn1, 16)
            sp.dma_start(kb2[:, :], column("L1_ffn_b2")).then_inc(w_ffn1, 16)
            sp.wait_ge(crow_ready, 1)
            for q in range(3):
                sp.dma_start(bias3[q:q + 1, 8 * D:9 * D], crow[:, :]).then_inc(crow_moved, 16)

            def body(r):
                p = r.parity
                if r.n < CHUNKS - 2 or r.k is not None:
                    sp.wait_ge(x_beta_ready, r.count(1, 1))
                    sp.wait_ge(xt_ps_ready, r.count(1, 1))
                    src = x_dram[r.n + 2] if r.k is None else x_dram[r.k * 2 + (r.n + 2)]
                    sp.dma_start(x_tok[p][:, :], src).then_inc(x_loaded[p], 16)
                if r.ffn1:
                    c = r - 3
                    sp.wait_ge(o_ready, c.count(1, 1))
                    dst = out_dram[c.n] if c.k is None else out_dram[c.k * 2 + c.n]
                    sp.dma_start(dst, o_tok[c.parity][:, :]).then_inc(out_stored[c.parity], 16)

            run_rounds(sp, body)
            for p in range(2):
                sp.wait_ge(out_stored[p], 16 * CHUNKS // 2)

        @block.gpsimd
        def _(pool):
            nc.gpsimd.memset(ident[:, :], 0.0).then_inc(pool_step, 1)
            pool.wait_ge(pool_step, 1)
            nc.gpsimd.affine_select(out=ident[:, :], in_=ident[:, :], compare_op=ALU.not_equal, fill=1.0, base=0,
                                    pattern=[[-1, 128]], channel_multiplier=1).then_inc(ident_ready, 1)
            for l in range(2):
                nc.gpsimd.memset(gates[l][:, 4 * B:5 * B], 0.0).then_inc(const_ready, 1)
            nc.gpsimd.memset(ones3[:, :], 1.0).then_inc(const_ready, 1)
            nc.gpsimd.memset(one_hot[:, :], 0.0).then_inc(const_ready, 1)
            nc.gpsimd.memset(minus_half[:, :], -0.5).then_inc(const_ready, 1)
            for k in range(KNOTS):
                nc.gpsimd.memset(kpos[:, k:k + 1], float(k)).then_inc(const_ready, 1)
                nc.gpsimd.memset(rank[:, k:k + 1], float(NC - k)).then_inc(const_ready, 1)
            pool.wait_ge(w_lstm1, 32)
            nc.gpsimd.tensor_scalar(wx[1][:, 0:3 * D], wx[1][:, 0:3 * D], 0.5, 1.0, ALU.mult, ALU.mult).then_inc(lstm_w_ready[1], 1)
            nc.gpsimd.tensor_scalar(wh[1][:, 0:3 * D], wh[1][:, 0:3 * D], 0.25, 1.0, ALU.mult, ALU.mult).then_inc(l1_split, 1)
            nc.gpsimd.tensor_scalar(wh[1][:, 3 * D:], wh[1][:, 3 * D:], 0.5, 1.0, ALU.mult, ALU.mult).then_inc(l1_split, 1)
            pool.wait_ge(l1_split, 2)
            nc.gpsimd.tensor_copy(whb[1][:, 0], wh[1][:, :]).then_inc(l1_split, 1)
            for q in (1, 2):
                pool.wait_ge(l1_split, 2 * q + 1)
                nc.gpsimd.tensor_tensor(wh[1][:, :], wh[1][:, :], whb[1][:, q - 1], ALU.subtract).then_inc(l1_split, 1)
                pool.wait_ge(l1_split, 2 * q + 2)
                nc.gpsimd.tensor_copy(whb[1][:, q], wh[1][:, :]).then_inc(l1_split, 1)
            pool.wait_ge(w_ffn0, 160)

            def third_part(l, c, s):
                pool.wait_ge(h_ready[l], c.count(STEPS, s + 1))
                hs = h[l][c.parity][:, s * B:(s + 1) * B]
                nc.gpsimd.tensor_tensor(h_rest[l][:, :], hs, hb[l][:, 0], ALU.subtract).then_inc(rest_ready[l], 1)
                pool.wait_ge(rest_ready[l], c.count(STEPS, s + 1))
                pool.wait_ge(part_ready[l][1], c.count(STEPS, s + 1))
                nc.gpsimd.tensor_tensor(hb[l][:, 2], h_rest[l][:, :], hb[l][:, 1], ALU.subtract).then_inc(part_ready[l][2], 1)

            def body(r):
                for s in range(STEPS):
                    if r.lstm0:
                        third_part(0, r, s)
                    pool_fill(r, s)
                    if r.lstm1:
                        third_part(1, r - 2, s)

            def pool_fill(r, s):
                c = r - 1
                q = c.parity
                if s == 0 and r.lstm0:
                    p = r.parity
                    if r.k is None and r.n == 0:
                        pool.wait_ge(x_loaded[0], 16)
                    else:
                        pool.wait_ge(x_loaded[p], r.pairs(16, 16))
                    if not (r.k is None and r.n < 2):
                        pool.wait_ge(x1_ready, r.count(1, -1))
                    nc.gpsimd.tensor_tensor(x_beta[p][:, :], x_tok[p][:, :], beta[:, :], ALU.add).then_inc(x_beta_ready, 1)
                if s == ONE_HOT_SLOT and r.ffn0:
                    pool.wait_ge(route, c.count(ROUTE, ROUTE))
                    if not (c.k is None and c.n == 0):
                        pool.wait_ge(one_hot_ps_ready, c.count(1))
                    nc.gpsimd.tensor_tensor(
                        one_hot[:, 0:NT].rearrange("p (c j) -> p c j", c=NC),
                        in_cluster[:, :].unsqueeze(2).to_broadcast([TOK, NC, TPC]),
                        in_local[:, :].unsqueeze(1).to_broadcast([TOK, NC, TPC]), ALU.mult).then_inc(one_hot_ready, 1)
                if s == 6 and r.ffn0:
                    pool.wait_ge(norm_step, c.count(4, 3))
                    nc.gpsimd.tensor_tensor(rstd[:, :], var_eps[:, :], minus_half[:, :], ALU.pow).then_inc(rstd_ready, 1)
                if s == 7 and r.ffn0:
                    pool.wait_ge(norm_step, c.count(4, 4))
                    nc.gpsimd.tensor_tensor(zg[:, :], z[:, :], gamma[:, :], ALU.mult).then_inc(zg_ready, 1)
                    pool.wait_ge(zg_ready, c.count(1, 1))
                    pool.wait_ge(x_beta_ready, c.count(1, 1))
                    if not (c.k is None and c.n < 2):
                        pool.wait_ge(o_ready, c.count(1, -1))
                    nc.gpsimd.tensor_tensor(x1_tok[q][:, :], zg[:, :], x_beta[q][:, :], ALU.add).then_inc(x1_ready, 1)

            run_rounds(pool, body)

        @block.tensor
        def _(pe):
            pe.wait_ge(ident_ready, 1)
            pe.wait_ge(x_loaded[0], 16)
            pe.transpose(turn_ps, x_tok[0][:, :], ident[:, :]).then_inc(xt_ps_ready, 1)
            pe.wait_ge(w_cond, 16)
            pe.transpose(ps_c[:, 0:B], cond[:, :], ident[0:B, 0:B]).then_inc(turned0, 1)
            pe.wait_ge(w_ffn0, 160)
            pe.transpose(ps_d[:, 0:NT], raw[:, :], ident[0:NT, 0:NT]).then_inc(turned0, 1)

            def bias_part(l, p):
                for q, g in enumerate(GATE):
                    pe.matmul(pre[l][p][:, q].rearrange("d s b -> d (s b)"), biasb[:, (4 * l + g) * D:(4 * l + g + 1) * D],
                              ones3[:, :], start=(q == 0), stop=False, skip_group_check=True)

            def x_part(l, p, src, q, s0, s1_):
                g = GATE[q]
                pe.matmul(pre[l][p][:, q, s0:s1_].rearrange("d s b -> d (s b)"), wx[l][:, g * D:(g + 1) * D],
                          src[:, s0 * B:s1_ * B], start=False, stop=False, skip_group_check=True)

            def h_part(l, c, s):
                p = c.parity
                for part in range(3):
                    if c.k is None and c.n == 0 and s == 0:
                        pe.wait_ge(start_ready, 6)
                    else:
                        pe.wait_ge(part_ready[l][part], c.count(STEPS, s))
                    for q, g in enumerate(GATE):
                        for wp in range(3 - part):
                            mm = pe.matmul(pre[l][p][:, q, s], whb[l][:, wp, g * D:(g + 1) * D], hb[l][:, part],
                                           start=False, stop=True, skip_group_check=True)
                mm.then_inc(pre_ready[l], 1)

            pe.wait_ge(bias_ready, 1)
            pe.wait_ge(const_ready, 5 + 2 * KNOTS)
            pe.wait_ge(lstm_w_ready[0], 2)
            pe.wait_ge(xt_ready, 1)
            bias_part(0, 0)
            for q in range(4):
                x_part(0, 0, x_t[0], q, 0, STEPS)
            pe.wait_ge(ffn1_w_ready, 1)
            pe.matmul(ps_d[0:1, 128:128 + D], kb2[:, :], wout2[0:M, :], start=True, stop=False)
            pe.matmul(ps_d[0:1, 128:128 + D], ident[0:1, 0:1], bout[:, :], start=False, stop=True).then_inc(crow_ps_ready, 1)

            def body(r):
                p = r.parity
                c0, c1 = r - 1, r - 3
                first = r.k is None
                for s in range(STEPS):
                    if r.lstm0:
                        h_part(0, r, s)
                    if s == 0 and r.ffn0:
                        if first and r.n == 1:
                            pe.wait_ge(ffn0_w_ready, 3)
                        pe.wait_ge(h_ready[0], c0.count(STEPS, STEPS))
                        if not (first and r.n == 1):
                            pe.wait_ge(tanhs_ready, c0.count(1))
                            pe.wait_ge(gelu_ready, c0.count(1))
                        hs = h[0][c0.parity]
                        pe.matmul(score_ps, hs[:, :], score_w[:, :], start=True, stop=True)
                        pe.matmul(compress_ps, comp_w1[:, :], hs[:, :], start=True, stop=True).then_inc(scores_ready, 1)
                    if r.lstm1 and s == 0:
                        if r.n == 2:
                            pe.wait_ge(l1_split, 7)
                        pe.wait_ge(x1t_ready, (r - 2).count(1, 1))
                        bias_part(1, p)
                        for q in range(4):
                            x_part(1, p, x1_t[p], q, 0, STEPS)
                    if r.lstm1:
                        h_part(1, r - 2, s)
                    if s == 0 and r.ffn1:
                        if r.n == 3:
                            pe.wait_ge(crow_split, 1)
                        pe.wait_ge(h_ready[1], c1.count(STEPS, STEPS))
                        if not (first and r.n == 3):
                            pe.wait_ge(o_ready, c1.count(1))
                        pe.matmul(ps_d[:, 0:TOK], win2[:, :], h[1][c1.parity][:, :], start=True, stop=True).then_inc(s1_ps_ready, 1)
                    if s == 1 and r.prepare:
                        pe.wait_ge(x_loaded[1 - p], (r - 0).pairs(16, 16) if p == 0 else (r - 0).pairs(16, 32))
                        if r.n >= 2:
                            pe.wait_ge(x1t_ready, r.count(1, -1))
                        elif r.n == 0:
                            pe.wait_ge(xt_ready, 1)
                        pe.transpose(turn_ps, x_tok[1 - p][:, :], ident[:, :]).then_inc(xt_ps_ready, 1)
                    if s == 2 and r.ffn0:
                        if r.prepare:
                            pe.wait_ge(xt_ready, r.count(1, 2))
                        pe.transpose(turn_ps, h[0][c0.parity][:, :], ident[:, :]).then_inc(h_tok_ps_ready, 1)
                    if s == 3 and r.ffn0:
                        pe.wait_ge(h_tok_ready, c0.count(1, 1))
                        pe.wait_ge(gelu_ready, c0.count(1, 1))
                        pe.matmul(ps_b[:, 0:2], gelu[:, :], comp_w2[:, :], start=True, stop=True).then_inc(comp_ps_ready, 1)
                    if s == 2 and r.prepare:
                        bias_part(0, 1 - p)
                    if s in (3, 4, 5, 6) and r.prepare:
                        if s == 3:
                            pe.wait_ge(xt_ready, r.count(1, 2))
                        x_part(0, 1 - p, x_t[1 - p], s - 3, 0, STEPS)
                    if s == 6 and r.ffn1:
                        pe.wait_ge(s1_ready, c1.count(1, 1))
                        pe.matmul(ps_d[:, 0:D], ones3[:, :], biasb[:, 8 * D:9 * D], start=True, stop=False)
                        pe.wait_ge(inner_step, c1.count(HALF, HALF))
                        pe.matmul(ps_d[:, 0:D], inner[:, :], wout2[:, :], start=False, stop=True).then_inc(ffn1_ps_ready, 1)
                    if s == 4 and r.ffn0:
                        pe.wait_ge(comp_ready, c0.count(1, 1))
                        pe.wait_ge(one_hot_ready, c0.count(1, 1))
                        pe.transpose(turn_ps, one_hot[:, :], ident[:, :]).then_inc(one_hot_ps_ready, 1)
                    if s == 5 and r.ffn0:
                        if first and r.n == 1:
                            pe.wait_ge(w_table, 80)
                        pe.wait_ge(one_hot_t_ready, c0.count(1, 1))
                        pe.matmul(ps_c[:, 0:C_ALL], one_hot_t[:, :], table[:, :], start=True, stop=True).then_inc(gathered, 1)
                    if s == 7 and r.ffn0:
                        pe.wait_ge(x1_ready, c0.count(1, 1))
                        pe.transpose(turn_ps, x1_tok[c0.parity][:, :], ident[:, :]).then_inc(x1t_ps_ready, 1)

            run_rounds(pe, body)

        @block.scalar
        def _(act):
            act.dma_start(cond[:, :], io["cond_1024"]).then_inc(w_cond, 16)
            for q in range(3):
                act.dma_start(bias3[q:q + 1, 0:4 * D], row("L0_cond_b")).then_inc(w_bias, 16)
                act.dma_start(bias3[q:q + 1, 4 * D:8 * D], row("L1_cond_b")).then_inc(w_bias, 16)
            act.dma_start(bout[:, :], row("L1_ffn_bout")).then_inc(w_bias, 16)
            act.wait_ge(const_ready, 5 + 2 * KNOTS)
            nc.scalar.activation(table_load[:, :], minus_half[:, :], ACT.Gelu).then_inc(table_loaded, 1)
            act.wait_ge(xt_ps_ready, 1)
            nc.scalar.activation(x_t[0][:, :], turn_ps, ACT.Identity).then_inc(xt_ready, 1)
            act.wait_ge(crow_ps_ready, 1)
            nc.scalar.activation(crow[:, :], ps_d[0:1, 128:128 + D], ACT.Identity).then_inc(crow_ready, 1)

            def gate_tanh(l, c, s):
                act.wait_ge(pre_ready[l], c.count(STEPS, s + 1))
                nc.scalar.activation(gates[l][:, 0:4 * B].rearrange("d (g b) -> d g b", g=4),
                                     pre[l][c.parity][:, :, s], ACT.Tanh).then_inc(gates_ready[l], 1)

            def cell_tanh_(l, c, s):
                act.wait_ge(cell_ready[l], c.count(STEPS, s + 1))
                nc.scalar.activation(cell_tanh[l][:, :], gates[l][:, 4 * B:5 * B], ACT.Tanh, scale=0.5).then_inc(tanh_ready[l], 1)

            def body(r):
                p = r.parity
                c0, c1 = r - 1, r - 3
                for s in range(STEPS):
                    if r.lstm0:
                        gate_tanh(0, r, s)
                    if s == 1 and r.ffn0:
                        if not (r.k is None and r.n == 1):
                            act.wait_ge(comp_ps_ready, c0.count(1))
                        nc.scalar.activation(gelu[0:CH, :], compress_ps, ACT.Gelu, bias=comp_b1[:, :]).then_inc(gelu_ready, 1)
                    if s == 5 and r.ffn0:
                        act.wait_ge(one_hot_ps_ready, c0.count(1, 1))
                        nc.scalar.activation(one_hot_t[:, :], ps_b[0:NT, 0:TOK], ACT.Identity).then_inc(one_hot_t_ready, 1)
                    if r.lstm0:
                        cell_tanh_(0, r, s)
                    if s == 0 and r.ffn0:
                        act.wait_ge(scores_ready, c0.count(1, 1))
                        nc.scalar.activation(tanhs[:, :], score_ps, ACT.Tanh, scale=half_inv_temp[:, :]).then_inc(tanhs_ready, 1)
                    if s in (1, 2, 3, 4) and r.ffn1:
                        if s == 1 and not (r.k is None and r.n == 3):
                            act.wait_ge(inner_step, c1.count(HALF))
                        act.wait_ge(s1_ready, c1.count(1, 1))
                        for j in (2 * s - 2, 2 * s - 1):
                            nc.scalar.activation(relus[:, j, :], s1[:, :], ACT.Relu, bias=kb1[:, j:j + 1],
                                                 scale=kw1[:, j:j + 1]).then_inc(relus_ready, 1)
                    if r.lstm1:
                        gate_tanh(1, r - 2, s)
                    if s == 0 and r.ffn1:
                        act.wait_ge(s1_ps_ready, c1.count(1, 1))
                        if r.n == 3:
                            act.wait_ge(ffn1_w_ready, 1)
                        nc.scalar.activation(s1[:, :], ps_d[:, 0:TOK], ACT.Identity, bias=bin2[:, :]).then_inc(s1_ready, 1)
                    if s == 1 and r.prepare:
                        act.wait_ge(xt_ps_ready, r.count(1, 2))
                        nc.scalar.activation(x_t[1 - p][:, :], turn_ps, ACT.Identity).then_inc(xt_ready, 1)
                    if s == 2 and r.ffn0:
                        act.wait_ge(h_tok_ps_ready, c0.count(1, 1))
                        nc.scalar.activation(h_tok[:, :], turn_ps, ACT.Identity).then_inc(h_tok_ready, 1)
                    if s == 3 and r.ffn0:
                        act.wait_ge(comp_ps_ready, c0.count(1, 1))
                        nc.scalar.activation(comp[:, :], ps_b[:, 0:2], ACT.Tanh).then_inc(comp_ready, 1)
                    if s == 5 and r.ffn0:
                        act.wait_ge(gathered, c0.count(1, 1))
                        nc.scalar.activation(spline[:, :], ps_c[:, 0:C_DIR], ACT.Identity).then_inc(spline_ready, 1)
                    if r.lstm1:
                        cell_tanh_(1, r - 2, s)
                    if s == 7 and r.ffn0:
                        act.wait_ge(x1t_ps_ready, c0.count(1, 1))
                        nc.scalar.activation(x1_t[c0.parity][:, :], turn_ps, ACT.Identity).then_inc(x1t_ready, 1)

            run_rounds(act, body)

        @block.vector
        def _(dve):
            dve.wait_ge(w_bias, 112)
            nc.vector.tensor_scalar(bias3[:, 0:3 * D], bias3[:, 0:3 * D], 0.5, None, ALU.mult).then_inc(set_dve, 1)
            nc.vector.tensor_scalar(bias3[:, 4 * D:7 * D], bias3[:, 4 * D:7 * D], 0.5, None, ALU.mult).then_inc(set_dve, 1)
            dve.wait_ge(set_dve, 2)

            steps = [2]

            def step(ins):
                steps[0] += 1
                ins.then_inc(set_dve, 1)
                dve.wait_ge(set_dve, steps[0])

            def split(c0_, c1_):
                w = slice(c0_, c1_)
                step(nc.vector.tensor_copy(part1[:, w], bias3[:, w]))
                step(nc.vector.tensor_tensor(rest[:, w], bias3[:, w], part1[:, w], ALU.subtract))
                step(nc.vector.tensor_copy(part2[:, w], rest[:, w]))
                step(nc.vector.tensor_tensor(rest[:, w], rest[:, w], part2[:, w], ALU.subtract))
                step(nc.vector.tensor_copy(part3[:, w], rest[:, w]))
                step(nc.vector.tensor_scalar(pick[:, w], part1[:, w], ident[0:3, 0:1], None, ALU.mult))
                step(nc.vector.scalar_tensor_tensor(out=pick[:, w], in0=part2[:, w], scalar=ident[0:3, 1:2], in1=pick[:, w],
                                                    op0=ALU.mult, op1=ALU.add))
                return nc.vector.scalar_tensor_tensor(out=biasb[:, w], in0=part3[:, w], scalar=ident[0:3, 2:3], in1=pick[:, w],
                                                      op0=ALU.mult, op1=ALU.add)

            dve.wait_ge(ident_ready, 1)
            split(0, 8 * D).then_inc(bias_ready, 1)
            dve.wait_ge(w_lstm0, 32)
            nc.vector.tensor_scalar(wx[0][:, 0:3 * D], wx[0][:, 0:3 * D], 0.5, None, ALU.mult).then_inc(lstm_w_ready[0], 1)
            nc.vector.tensor_scalar(wh[0][:, 3 * D:], wh[0][:, 3 * D:], 0.5, None, ALU.mult)
            step(nc.vector.tensor_scalar(wh[0][:, 0:3 * D], wh[0][:, 0:3 * D], 0.25, None, ALU.mult))
            step(nc.vector.tensor_copy(whb[0][:, 0], wh[0][:, :]))
            step(nc.vector.tensor_tensor(wh[0][:, :], wh[0][:, :], whb[0][:, 0], ALU.subtract))
            step(nc.vector.tensor_copy(whb[0][:, 1], wh[0][:, :]))
            step(nc.vector.tensor_tensor(wh[0][:, :], wh[0][:, :], whb[0][:, 1], ALU.subtract))
            nc.vector.tensor_copy(whb[0][:, 2], wh[0][:, :]).then_inc(lstm_w_ready[0], 1)
            dve.wait_ge(turned0, 1)
            start = h[0][1][:, TOK - B:TOK]
            step(nc.vector.tensor_scalar(start, ps_c[:, 0:B], 2.0, None, ALU.mult))
            for q in range(3):
                for l in range(2):
                    last = nc.vector.tensor_copy(hb[l][:, q], start)
                    last.then_inc(start_ready, 1)
                if q < 2:
                    dve.wait_ge(start_ready, 2 * q + 2)
                    step(nc.vector.tensor_tensor(start, start, hb[0][:, q], ALU.subtract))
            dve.wait_ge(turned0, 2)
            step(nc.vector.tensor_copy(sig_raw[:, :], ps_d[:, 0:NT]))
            step(nc.vector.tensor_scalar(sig_a[:, :], sig_raw[:, :], -0.3, -1.0, ALU.is_lt, ALU.mult))
            step(nc.vector.scalar_tensor_tensor(out=sig_q[:, :], in0=sig_raw[:, :], scalar=0.3, in1=sig_a[:, :],
                                                op0=ALU.is_gt, op1=ALU.add))
            step(nc.vector.tensor_tensor(sig_a[:, :], sig_q[:, :], sig_raw[:, :], ALU.subtract))
            step(nc.vector.tensor_tensor(sig_t[:, :], sig_raw[:, :], sig_a[:, :], ALU.add))
            tiles = sig_t[:, :].rearrange("d (c j) -> d c j", c=NC)
            step(nc.vector.tensor_tensor(csum[:, 1], tiles[:, :, 0], tiles[:, :, 1], ALU.add))
            for j in range(2, TPC):
                step(nc.vector.tensor_tensor(csum[:, j % 2], csum[:, (j + 1) % 2], tiles[:, :, j], ALU.add))
            total = csum[:, (TPC - 1) % 2]
            step(nc.vector.tensor_scalar(cneg[:, :], total, 0.0, 0.5, ALU.is_lt, ALU.mult))
            nc.vector.tensor_scalar(score_w[:, NC:], sig_t[:, :], 0.5, None, ALU.mult)
            step(nc.vector.tensor_scalar(csum[:, TPC % 2], total, 0.0, 0.5, ALU.is_gt, ALU.mult))
            nc.vector.tensor_tensor(score_w[:, 0:NC], csum[:, TPC % 2], cneg[:, :], ALU.subtract).then_inc(ffn0_w_ready, 1)
            nc.vector.tensor_scalar(comp_w1[:, :], comp_w1[:, :], 0.5, None, ALU.mult)
            nc.vector.tensor_scalar(scale2[:, :], scale2[:, :], 2.0, None, ALU.mult)
            nc.vector.memset(slopes[:, KNOTS - 1:KNOTS], 0.0)
            nc.vector.memset(gelu[CH:CH + 1, :], 1.0)
            nc.vector.tensor_tensor(slopes[:, 0:KNOTS - 1], knots[:, 1:KNOTS], knots[:, 0:KNOTS - 1], ALU.subtract).then_inc(ffn0_w_ready, 1)
            step(nc.vector.tensor_scalar(temp[:, :], temp[:, :], 1e-6, None, ALU.add))
            step(nc.vector.reciprocal(half_inv_temp[:, :], temp[:, :]))
            nc.vector.tensor_scalar(half_inv_temp[:, :], half_inv_temp[:, :], 0.5, None, ALU.mult).then_inc(ffn0_w_ready, 1)
            dve.wait_ge(w_ffn1, 208)
            nc.vector.tensor_scalar(win2[:, :], win2[:, :], 0.5, None, ALU.mult).then_inc(ffn1_w_ready, 1)
            dve.wait_ge(const_ready, 5 + 2 * KNOTS)

            def lstm_cell(l, c, s):
                n = c.count(STEPS, s + 1)
                dve.wait_ge(gates_ready[l], n)
                nc.vector.scalar_tensor_tensor(out=mixed[l][:, :], in0=gates[l][:, B:3 * B], scalar=1.0, in1=gates[l][:, 3 * B:5 * B],
                                               op0=ALU.add, op1=ALU.mult).then_inc(mixed_ready[l], 1)
                dve.wait_ge(mixed_ready[l], n)
                nc.vector.scalar_tensor_tensor(out=gates[l][:, 4 * B:5 * B], in0=mixed[l][:, B:2 * B], scalar=0.5,
                                               in1=mixed[l][:, 0:B], op0=ALU.mult, op1=ALU.add).then_inc(cell_ready[l], 1)

            def lstm_h(l, c, s):
                dve.wait_ge(tanh_ready[l], c.count(STEPS, s + 1))
                nc.vector.scalar_tensor_tensor(out=hb[l][:, 0], in0=gates[l][:, 0:B], scalar=1.0,
                                               in1=cell_tanh[l][:, :], op0=ALU.add, op1=ALU.mult).then_inc(part_ready[l][0], 1)
                hs = h[l][c.parity][:, s * B:(s + 1) * B]
                nc.vector.scalar_tensor_tensor(out=hs, in0=gates[l][:, 0:B], scalar=1.0,
                                               in1=cell_tanh[l][:, :], op0=ALU.add, op1=ALU.mult).then_inc(h_ready[l], 1)
                dve.wait_ge(h_ready[l], c.count(STEPS, s + 1))
                nc.vector.tensor_tensor(hb[l][:, 1], hs, hb[l][:, 0], ALU.subtract).then_inc(part_ready[l][1], 1)

            def wide(ap):
                return ap.unsqueeze(2).to_broadcast([TOK, NC, KNOTS])

            def knotwise(ap):
                return ap[:, :].unsqueeze(1).to_broadcast([TOK, NC, KNOTS])

            away3 = away[:, :].rearrange("p (c k) -> p c k", c=NC)
            seg3 = seg[:, :].rearrange("p (c k) -> p c k", c=NC)

            def calibrate(src, c, n, i):
                dve.wait_ge(route, c.count(ROUTE, n))
                if i == 0:
                    ins = nc.vector.scalar_tensor_tensor(out=away3, in0=wide(src), scalar=float(KNOTS - 1), in1=knotwise(kpos),
                                                         op0=ALU.mult, op1=ALU.subtract)
                if i == 1:
                    ins = nc.vector.tensor_tensor(seg3, away3, knotwise(slopes), ALU.mult)
                if i == 2:
                    ins = nc.vector.tensor_tensor(seg3, seg3, knotwise(knots), ALU.add)
                if i == 3:
                    ins = nc.vector.scalar_tensor_tensor(out=seg3, in0=away3, scalar=1.0, in1=seg3, op0=ALU.is_lt, op1=ALU.mult)
                if i == 4:
                    ins = nc.vector.scalar_tensor_tensor(out=seg3, in0=away3, scalar=0.0, in1=seg3, op0=ALU.is_ge, op1=ALU.mult)
                if i == 5:
                    ins = nc.vector.tensor_reduce(gate_v[:, :], seg3, AX_X, ALU.add)
                ins.then_inc(route, 1)

            def first_of_largest(dst, c, n, i):
                dve.wait_ge(route, c.count(ROUTE, n))
                if i == 0:
                    ins = nc.vector.tensor_reduce(gate_m[:, :], gate_v[:, :], AX_X, ALU.max)
                if i == 1:
                    ins = nc.vector.scalar_tensor_tensor(out=ranks[:, :], in0=gate_v[:, :], scalar=gate_m[:, :], in1=rank[:, :],
                                                         op0=ALU.is_equal, op1=ALU.mult)
                if i == 2:
                    ins = nc.vector.tensor_reduce(rank_m[:, :], ranks[:, :], AX_X, ALU.max)
                if i == 3:
                    ins = nc.vector.tensor_scalar(dst[:, :], rank[:, :], rank_m[:, :], None, ALU.is_equal)
                ins.then_inc(route, 1)

            def route_step(c, n):
                if n == 0:
                    dve.wait_ge(tanhs_ready, c.count(1, 1))
                    if not (c.k is None and c.n == 0):
                        dve.wait_ge(one_hot_ready, c.count(1))
                    nc.vector.tensor_scalar(sigm[:, :], tanhs[:, :], 0.5, 0.5, ALU.mult, ALU.add).then_inc(route, 1)
                elif n < 7:
                    calibrate(sigm[:, 0:NC], c, n, n - 1)
                elif n < 11:
                    first_of_largest(in_cluster, c, n, n - 7)
                elif n == 11:
                    dve.wait_ge(route, c.count(ROUTE, 11))
                    nc.vector.tensor_tensor(sel[:, :].rearrange("p (j c) -> p c j", j=TPC),
                                            sigm[:, NC:].rearrange("p (c j) -> p c j", c=NC),
                                            in_cluster[:, :].unsqueeze(2).to_broadcast([TOK, NC, TPC]),
                                            ALU.mult).then_inc(route, 1)
                elif n == 12:
                    dve.wait_ge(route, c.count(ROUTE, 12))
                    nc.vector.tensor_reduce(picked[:, :], sel[:, :].rearrange("p (j c) -> p j c", j=TPC), AX_X,
                                            ALU.add).then_inc(route, 1)
                elif n < 19:
                    calibrate(picked[:, :], c, n, n - 13)
                else:
                    first_of_largest(in_local, c, n, n - 19)

            def inner_sum(c, j):
                dve.wait_ge(relus_ready, c.count(HALF, j + 1))
                if j == 0:
                    if not (c.k is None and c.n == 0):
                        dve.wait_ge(ffn1_ps_ready, c.count(1))
                    nc.vector.tensor_scalar(inner[:, :], relus[:, 0, :], kw2[:, 0:1], None, ALU.mult).then_inc(inner_step, 1)
                else:
                    dve.wait_ge(inner_step, c.count(HALF, j))
                    nc.vector.scalar_tensor_tensor(out=inner[:, :], in0=relus[:, j, :], scalar=kw2[:, j:j + 1], in1=inner[:, :],
                                                   op0=ALU.mult, op1=ALU.add).then_inc(inner_step, 1)

            def spline_step(c, n):
                if n == 0:
                    dve.wait_ge(spline_ready, c.count(1, 1))
                    dve.wait_ge(comp_ready, c.count(1, 1))
                    nc.vector.scalar_tensor_tensor(out=hidden[:, :], in0=spline[:, 0:GRID], scalar=comp[:, 0:1],
                                                   in1=spline[:, C_B1:C_W2], op0=ALU.mult, op1=ALU.add).then_inc(mag_step, 1)
                if n == 1:
                    dve.wait_ge(mag_step, c.count(5, 1))
                    nc.vector.scalar_tensor_tensor(out=hidden2[:, :], in0=spline[:, GRID:2 * GRID], scalar=comp[:, 1:2],
                                                   in1=hidden[:, :], op0=ALU.mult, op1=ALU.add).then_inc(mag_step, 1)
                if n == 2:
                    dve.wait_ge(mag_step, c.count(5, 2))
                    nc.vector.scalar_tensor_tensor(out=hidden3[:, :], in0=hidden2[:, :], scalar=0.0, in1=spline[:, C_W2:C_B2],
                                                   op0=ALU.max, op1=ALU.mult, accum_out=mag[:, :]).then_inc(mag_step, 1)
                if n == 3:
                    dve.wait_ge(mag_step, c.count(5, 3))
                    nc.vector.tensor_scalar(mag2[:, :], mag[:, :], spline[:, C_B2:C_DIR], scale2[:, :],
                                            ALU.add, ALU.mult).then_inc(mag_step, 1)
                if n == 4:
                    dve.wait_ge(mag_step, c.count(5, 4))
                    dve.wait_ge(h_tok_ready, c.count(1, 1))
                    nc.vector.scalar_tensor_tensor(out=y2[:, :], in0=ps_c[:, C_DIR:C_ALL], scalar=mag2[:, :], in1=h_tok[:, :],
                                                   op0=ALU.mult, op1=ALU.add).then_inc(mag_step, 1)
                if n == 5:
                    dve.wait_ge(mag_step, c.count(5, 5))
                    nc.vector.bn_stats(stats[:, :], y2[:, :]).then_inc(norm_step, 1)
                if n == 6:
                    dve.wait_ge(norm_step, c.count(4, 2))
                    nc.vector.tensor_scalar(var_eps[:, :], mean_var[:, 1:2], 4.0 * EPS_LN, None, ALU.add).then_inc(norm_step, 1)
                if n == 7:
                    dve.wait_ge(rstd_ready, c.count(1, 1))
                    nc.vector.tensor_scalar(z[:, :], y2[:, :], mean_var[:, 0:1], rstd[:, :], ALU.subtract, ALU.mult).then_inc(norm_step, 1)

            def fill(r, place):
                c0, c1 = r - 1, r - 3
                first = 2 * (place - ROUTE_AT)
                if r.ffn0:
                    if 0 <= first < ROUTE:
                        route_step(c0, first)
                if r.ffn1 and INNER_AT <= place < INNER_AT + 2 * HALF and (place - INNER_AT) % 2 == 0:
                    inner_sum(c1, (place - INNER_AT) // 2)
                if r.ffn0:
                    if 0 <= first < ROUTE - 1:
                        route_step(c0, first + 1)
                    for n, at in enumerate(SPLINE_AT):
                        if place == at:
                            spline_step(c0, n)

            def body(r):
                c0, c1 = r - 1, r - 3
                for s in range(STEPS):
                    if r.lstm0:
                        lstm_cell(0, r, s)
                    fill(r, 4 * s)
                    if r.lstm0:
                        lstm_h(0, r, s)
                    fill(r, 4 * s + 1)
                    if r.lstm1:
                        lstm_cell(1, r - 2, s)
                    fill(r, 4 * s + 2)
                    if s == AGGR_SLOT and r.ffn0:
                        dve.wait_ge(norm_step, c0.count(4, 1))
                    if r.lstm1:
                        lstm_h(1, r - 2, s)
                    if s == AGGR_SLOT and r.ffn0:
                        nc.vector.bn_aggr(mean_var[:, :], stats[:, :]).then_inc(norm_step, 1)
                    fill(r, 4 * s + 3)
                    if s == 7 and r.ffn1:
                        dve.wait_ge(ffn1_ps_ready, c1.count(1, 1))
                        if not (r.k is None and r.n < 5):
                            dve.wait_ge(out_stored[c1.parity], c1.pairs(16))
                        nc.vector.tensor_tensor(o_tok[c1.parity][:, :], ps_d[:, 0:D], x1_tok[c1.parity][:, :], ALU.add).then_inc(o_ready, 1)
                if r.k is None and r.n == 2:
                    dve.wait_ge(crow_moved, 48)
                    split(8 * D, 9 * D).then_inc(crow_split, 1)

            run_rounds(dve, body)


_INS = ['x', 'cond_1024', 'L0_cond_Wx', 'L0_cond_Wh', 'L0_cond_b', 'L0_ffn_signatures_raw', 'L0_ffn_knot_values',
        'L0_ffn_temperature', 'L0_ffn_compress_w1', 'L0_ffn_compress_b1', 'L0_ffn_compress_w2', 'L0_ffn_compress_b2',
        'L0_ffn_spline_w1', 'L0_ffn_spline_b1', 'L0_ffn_spline_w2', 'L0_ffn_spline_b2', 'L0_ffn_directions',
        'L0_ffn_norm_gamma', 'L0_ffn_norm_beta', 'L0_ffn_output_scale', 'L1_cond_Wx', 'L1_cond_Wh', 'L1_cond_b',
        'L1_ffn_Win', 'L1_ffn_bin_', 'L1_ffn_W1', 'L1_ffn_b1', 'L1_ffn_W2', 'L1_ffn_b2', 'L1_ffn_Wout', 'L1_ffn_bout']


def kernel(**inputs):
    import numpy as _np
    import concourse.bacc as _bacc
    from concourse import mybir as _mybir
    from concourse.bass_utils import run_bass_kernel_spmd as _run

    nc = _bacc.Bacc("TRN2", target_bir_lowering=False, num_devices=1)
    arrays, io = {}, {}
    for name in _INS:
        a = _np.ascontiguousarray(inputs[name])
        arrays[f"in_{name}"] = a
        io[name] = nc.dram_tensor(f"in_{name}", a.shape, _mybir.dt.from_np(a.dtype), kind="ExternalInput").ap()
    out = nc.dram_tensor("out_x", (B, T, D), _mybir.dt.float32, kind="ExternalOutput").ap()
    build(nc, io, out)
    r = _run(nc, [arrays], core_ids=[0])
    return r.results[0]["out_x"]
```

```python
from contextlib import ExitStack

import numpy as np

import concourse.bass as bass
from concourse import mybir

ALU = mybir.AluOpType
ACT = mybir.ActivationFunctionType
F32 = mybir.dt.float32
BF16 = mybir.dt.bfloat16
AX_X = mybir.AxisListType.X

B, T, D = 16, 128, 128
STEPS = 8
TOK = STEPS * B
CHUNKS = T // STEPS
NT, NC, TPC = 64, 8, 8
KNOTS = 8
CH = 32
GRID = 16
M, INNER = 64, 16
HALF = INNER // 2
GATE = [2, 0, 1, 3]
EPS_LN = 1e-5

C_W1, C_B1, C_W2, C_B2, C_DIR = 0, 2 * GRID, 3 * GRID, 4 * GRID, 4 * GRID + 1
C_ALL = C_DIR + D
SCORES = NC + NT

A_COMP = 4 * D
A_LSTM = [0, 4 * D + CH]
A_ALL = 8 * D + CH

ROUNDS = CHUNKS + 4
LOOP_FROM, LOOP_TRIPS, PER_TRIP = 6, 2, 4
LAG1 = 2

ROUTE = 23
ROUTE_AT = [(1, 1), (1, 2), (1, 3), (2, 0), (2, 1), (2, 2), (2, 3), (3, 0), (3, 1), (3, 2), (3, 3), (4, 0), (4, 1),
            (4, 2), (5, 0), (5, 1), (5, 1), (5, 2), (6, 0), (6, 1), (6, 1), (6, 2), (7, 0), (7, 1), (7, 1)]
SPLINE_AT = [(9, 1), (9, 2), (9, 3), (10, 0), (10, 1), (10, 2), (11, 1), (12, 0), (12, 1)]
AGGREGATE_AT = 11
INNER_AT = [(12, 2), (13, 1), (13, 3), (14, 1), (15, 1), (16, 1), (17, 1), (18, 1)]
OUT_AT = (4, 1)
L0_X_AT = [10, 11, 12, 13]
L1_X_AT = [15, 17, 18, 19]
TURN_H_AT = [5, 6, 7]
FFN1_END_AT, TURN_X_AT, FFN1_IN_AT = 4, 5, [6, 7]
TURN_TILE_AT, GATHER_AT, TURN_X1_AT = 8, 9, 14
TANHS_AT, GELU_AT, X_T_AT, S1_AT = (1, 0), (1, 1), (5, 0), (7, 0)
H_TOK_AT, TILE_T_AT, SPLINE_ROW_AT, X1_T_AT = (8, 0), (8, 0), (9, 0), (14, 0)
RELU_AT = [(10, 0), (10, 1), (11, 0), (12, 0), (13, 0), (14, 0), (15, 0), (16, 0)]
TILE_AT, RSTD_AT, KEEP_AT, X_BETA_AT = (7, 0), (11, 0), (8, 1), (10, 1)


def steps_at(places, half, which):
    return [n for n, place in enumerate(places) if place == (half, which)]


class Chunk:

    def __init__(self, k, n):
        self.k, self.n, self.parity = k, n, n % 2

    def __sub__(self, m):
        return Chunk(self.k, self.n - m)

    @property
    def real(self):
        return self.k is not None or 0 <= self.n < CHUNKS

    @property
    def first(self):
        return self.k is None and self.n == 0

    def index(self, more=0):
        return self.n + more if self.k is None else self.k * PER_TRIP + (self.n + more)

    def count(self, per_chunk, more=0):
        v = self.n * per_chunk + more
        return v if self.k is None else self.k * (PER_TRIP * per_chunk) + v

    def pairs(self, per_pair, more=0):
        v = (self.n // 2) * per_pair + more
        return v if self.k is None else self.k * (PER_TRIP // 2 * per_pair) + v


def lstm1_step(r, s):
    return (r - 3, s + STEPS - LAG1) if s < LAG1 else (r - 2, s - LAG1)


def run_rounds(engine, body):
    for n in range(LOOP_FROM):
        body(Chunk(None, n))
    if LOOP_TRIPS:
        with engine.Fori(0, LOOP_TRIPS) as k:
            for n in range(PER_TRIP):
                body(Chunk(k, LOOP_FROM + n))
    for n in range(LOOP_FROM + PER_TRIP * LOOP_TRIPS, ROUNDS):
        body(Chunk(None, n))


def build(nc, io, out):
    with ExitStack() as ctx:
        def sb(name, shape, dt=F32):
            return ctx.enter_context(nc.sbuf_tensor(name, shape, dt))

        def ps(name, shape):
            return ctx.enter_context(nc.psum_tensor(name, shape, F32))

        def sem(name):
            return ctx.enter_context(nc.semaphore(name))

        wx = [sb(f"wx{l}", [D, 4 * D]) for l in range(2)]
        wh = [sb(f"wh{l}", [D, 4 * D]) for l in range(2)]
        whb = [sb(f"whb{l}", [D, 3, 4 * D], BF16) for l in range(2)]
        bias3 = sb("bias3", [3, A_ALL])
        bias_p = sb("bias_p", [3, 4 * D + CH], BF16)
        bias_r = sb("bias_r", [3, 4 * D + CH])
        biasb = sb("biasb", [3, A_ALL], BF16)
        later = sb("later", [3, 2])
        ones3 = sb("ones3", [3, TOK], BF16)
        ones1 = sb("ones1", [1, TOK])
        identb = sb("identb", [128, 128], BF16)
        ident = sb("ident", [128, 128])
        cond = sb("cond", [B, D])
        raw = sb("raw", [NT, D])
        sig_raw = sb("sig_raw", [D, NT])
        sig_a = sb("sig_a", [D, NT])
        sig_q = sb("sig_q", [D, NT])
        sig_t = sb("sig_t", [D, NT])
        csum = sb("csum", [D, 2, NC])
        cneg = sb("cneg", [D, NC])
        score_w = sb("score_w", [D, SCORES + CH])
        score_r = sb("score_r", [D, SCORES + CH])
        score_wb = sb("score_wb", [D, 3, SCORES + CH], BF16)
        comp_w2 = sb("comp_w2", [128, 2 * (CH + 1)])
        temp = sb("temp", [128, 1])
        half_inv_temp = sb("half_inv_temp", [128, 1])
        knots = sb("knots", [128, KNOTS])
        slopes = sb("slopes", [128, KNOTS])
        kpos = sb("kpos", [128, KNOTS])
        rank = sb("rank", [128, NC])
        scale2 = sb("scale2", [128, 1])
        gamma = sb("gamma", [128, D])
        beta = sb("beta", [128, D])
        table = sb("table", [NT, C_ALL])
        table_r = sb("table_r", [NT, C_ALL])
        tableb = sb("tableb", [NT, 3, C_ALL], BF16)
        win2 = sb("win2", [D, 2 * M])
        win2_r = sb("win2_r", [D, 2 * M])
        win2b = sb("win2b", [D, 3, 2 * M], BF16)
        bin2 = sb("bin2", [2 * M, 1])
        kw1 = sb("kw1", [2 * M, HALF])
        kb1 = sb("kb1", [2 * M, HALF])
        kw2 = sb("kw2", [2 * M, HALF])
        kb2 = sb("kb2", [M, 1])
        wout2 = sb("wout2", [2 * M, D])
        bout = sb("bout", [1, D])
        ffn1_const = sb("ffn1_const", [TOK, D])
        table_load = sb("table_load", [128, 1])
        minus_half = sb("minus_half", [128, 1])

        x_tok = [sb(f"x_tok{p}", [TOK, D]) for p in range(2)]
        x_t = [sb(f"x_t{p}", [D, TOK]) for p in range(2)]
        x_beta = [sb(f"x_beta{p}", [TOK, D]) for p in range(2)]
        hb = [[sb(f"hb{l}_{p}", [D, 3, TOK], BF16) for p in range(2)] for l in range(2)]
        start = sb("start", [D, B])
        h_now = [sb(f"h_now{l}", [D, B]) for l in range(2)]
        h_rest = [sb(f"h_rest{l}", [D, B]) for l in range(2)]
        gates = [sb(f"gates{l}", [D, 5 * B]) for l in range(2)]
        mixed = [sb(f"mixed{l}", [D, 2 * B]) for l in range(2)]
        cell_tanh = [sb(f"cell_tanh{l}", [D, B]) for l in range(2)]
        tanhs = sb("tanhs", [TOK, NC + NT])
        sigm = sb("sigm", [TOK, NC + NT])
        picked = sb("picked", [TOK, TPC])
        away = sb("away", [TOK, NC * KNOTS])
        seg = sb("seg", [TOK, NC * KNOTS])
        gate_v = sb("gate_v", [TOK, NC])
        gate_m = sb("gate_m", [TOK, 1])
        ranks = sb("ranks", [TOK, NC])
        rank_m = sb("rank_m", [TOK, 1])
        in_cluster = sb("in_cluster", [TOK, NC])
        in_local = sb("in_local", [TOK, TPC])
        sel = sb("sel", [TOK, NT])
        one_hot = sb("one_hot", [TOK, 128], BF16)
        one_hot_t = sb("one_hot_t", [NT, TOK], BF16)
        spline = sb("spline", [TOK, C_DIR])
        gelu = sb("gelu", [TOK, CH + 1])
        gelu_w = sb("gelu_w", [TOK, 2, CH + 1])
        comp_sum = sb("comp_sum", [TOK, 2])
        comp = sb("comp", [TOK, 2])
        hidden = sb("hidden", [TOK, GRID])
        hidden2 = sb("hidden2", [TOK, GRID])
        hidden3 = sb("hidden3", [TOK, GRID])
        mag = sb("mag", [TOK, 1])
        mag2 = sb("mag2", [TOK, 1])
        h_tok = sb("h_tok", [TOK, D])
        y2 = sb("y2", [TOK, D])
        stats = sb("stats", [TOK, 6])
        mean_var = sb("mean_var", [TOK, 2])
        var_eps = sb("var_eps", [TOK, 1])
        rstd = sb("rstd", [TOK, 1])
        centred = sb("centred", [TOK, D])
        x1_tok = sb("x1_tok", [TOK, D])
        x1_keep = [sb(f"x1_keep{p}", [TOK, D]) for p in range(2)]
        x1_t = sb("x1_t", [D, TOK])
        s1 = sb("s1", [2 * M, TOK])
        relus = sb("relus", [2 * M, HALF, TOK])
        inner = sb("inner", [2 * M, TOK])
        o_tok = [sb(f"o_tok{p}", [TOK, D]) for p in range(2)]

        pre = [[ps(f"pre{l}_{p}", [D, 4, STEPS, B]) for p in range(2)] for l in range(2)]
        ps_a = ps("ps_a", [128, 512])
        ps_b = ps("ps_b", [128, 512])
        ps_c = ps("ps_c", [128, 512])
        ps_d = ps("ps_d", [128, 512])
        turn_ps, h_tok_ps = ps_b[:, 0:128], ps_c[:, 256:256 + D]

        w_lstm0_x = sem("w_lstm0_x")
        w_lstm0, w_lstm1, w_ffn0, w_ffn1 = sem("w_lstm0"), sem("w_lstm1"), sem("w_ffn0"), sem("w_ffn1")
        table_loaded = sem("table_loaded")
        w_bias0, w_bias, w_bias1, w_cond, w_table = sem("w_bias0"), sem("w_bias"), sem("w_bias1"), sem("w_cond"), sem("w_table")
        x_loaded = [sem(f"x_loaded{p}") for p in range(2)]
        out_stored = [sem(f"out_stored{p}") for p in range(2)]
        const_ready = sem("const_ready")
        pool_step = sem("pool_step")
        ident_ready = sem("ident_ready")
        turned0 = sem("turned0")
        set_dve = sem("set_dve")
        wx0_ready, lstm0_w_ready = sem("wx0_ready"), sem("lstm0_w_ready")
        l1_scaled, l1_rest, l1_w_ready = sem("l1_scaled"), sem("l1_rest"), sem("l1_w_ready")
        identb_ready = sem("identb_ready")
        start_ready = sem("start_ready")
        bias0_row_ready, bias0_ready, bias1_ready = sem("bias0_row_ready"), sem("bias0_ready"), sem("bias1_ready")
        score_w_ready, temp_ready, table_ready = sem("score_w_ready"), sem("temp_ready"), sem("table_ready")
        ffn1_w_ready = sem("ffn1_w_ready")
        const_ps_ready, ffn1_const_ready = sem("const_ps_ready"), sem("ffn1_const_ready")
        pre_ready = [sem(f"pre_ready{l}") for l in range(2)]
        gates_ready = [sem(f"gates_ready{l}") for l in range(2)]
        mixed_ready = [sem(f"mixed_ready{l}") for l in range(2)]
        cell_ready = [sem(f"cell_ready{l}") for l in range(2)]
        tanh_ready = [sem(f"tanh_ready{l}") for l in range(2)]
        h_ready = [sem(f"h_ready{l}") for l in range(2)]
        part_ready = [[sem(f"part{q}_ready{l}") for q in range(3)] for l in range(2)]
        rest_ready = [sem(f"rest_ready{l}") for l in range(2)]
        xt_ps_ready, xt_ready, x_beta_ready = sem("xt_ps_ready"), sem("xt_ready"), sem("x_beta_ready")
        scores_ready, tanhs_ready = sem("scores_ready"), sem("tanhs_ready")
        gelu_ready = sem("gelu_ready")
        comp_summed, comp_ready = sem("comp_summed"), sem("comp_ready")
        route = sem("route")
        one_hot_ready, one_hot_ps_ready, one_hot_t_ready = sem("one_hot_ready"), sem("one_hot_ps_ready"), sem("one_hot_t_ready")
        gathered, spline_ready = sem("gathered"), sem("spline_ready")
        h_tok_ps_ready, h_tok_ready = sem("h_tok_ps_ready"), sem("h_tok_ready")
        mag_step = sem("mag_step")
        norm_step = sem("norm_step")
        rstd_ready = sem("rstd_ready")
        x1_ready, x1_kept = sem("x1_ready"), sem("x1_kept")
        x1t_ps_ready, x1t_ready = sem("x1t_ps_ready"), sem("x1t_ready")
        s1_ps_ready, s1_ready, relus_ready = sem("s1_ps_ready"), sem("s1_ready"), sem("relus_ready")
        inner_step = sem("inner_step")
        ffn1_ps_ready, o_ready = sem("ffn1_ps_ready"), sem("o_ready")

        x_dram = io["x"].rearrange("b (c t) d -> c t b d", t=STEPS)
        out_dram = out.rearrange("b (c t) d -> c t b d", t=STEPS)

        def row(name):
            return io[name].rearrange("(a d) -> a d", a=1)

        def column(name):
            return io[name].rearrange("(d a) -> d a", a=1)

        block = ctx.enter_context(nc.Block())

        @block.sync
        def _(sp):
            sp.dma_start(wh[0][:, :], io["L0_cond_Wh"]).then_inc(w_lstm0, 16)
            sp.dma_start(x_tok[0][:, :], x_dram[0]).then_inc(x_loaded[0], 16)
            sp.dma_start(cond[:, :], io["cond_1024"]).then_inc(w_cond, 16)
            sp.dma_start(x_tok[1][:, :], x_dram[1]).then_inc(x_loaded[1], 16)
            sp.dma_start(bias3[:, A_COMP:A_COMP + CH], row("L0_ffn_compress_b1").to_broadcast([3, CH])).then_inc(w_bias, 16)
            sp.dma_start(raw[:, :], io["L0_ffn_signatures_raw"]).then_inc(w_ffn0, 16)
            sp.dma_start(score_w[:, SCORES:], io["L0_ffn_compress_w1"]).then_inc(w_ffn0, 16)
            sp.dma_start(comp_w2[:, 0:2 * CH], io["L0_ffn_compress_w2"].rearrange("(a i) o -> a (i o)", a=1)
                         .to_broadcast([128, 2 * CH])).then_inc(w_ffn0, 16)
            sp.dma_start(comp_w2[:, 2 * CH:], row("L0_ffn_compress_b2").to_broadcast([128, 2])).then_inc(w_ffn0, 16)
            sp.dma_start(knots[:, :], row("L0_ffn_knot_values").to_broadcast([128, KNOTS])).then_inc(w_ffn0, 16)
            sp.dma_start(temp[:, :], row("L0_ffn_temperature").to_broadcast([128, 1])).then_inc(w_ffn0, 16)
            sp.dma_start(scale2[:, :], row("L0_ffn_output_scale").to_broadcast([128, 1])).then_inc(w_ffn0, 16)
            sp.dma_start(beta[:, :], row("L0_ffn_norm_beta").to_broadcast([128, D])).then_inc(w_ffn0, 16)
            sp.dma_start(gamma[:, :], row("L0_ffn_norm_gamma").to_broadcast([128, D])).then_inc(w_ffn0, 16)
            sp.dma_start(wh[1][:, :], io["L1_cond_Wh"]).then_inc(w_lstm1, 16)
            sp.dma_start(wx[1][:, :], io["L1_cond_Wx"]).then_inc(w_lstm1, 16)
            sp.dma_start(bias3[:, A_LSTM[1]:A_LSTM[1] + 4 * D], row("L1_cond_b").to_broadcast([3, 4 * D])).then_inc(w_bias1, 16)
            sp.dma_start(table[:, C_W1:C_B1], io["L0_ffn_spline_w1"].rearrange("n i g -> n (i g)")).then_inc(w_table, 16)
            sp.dma_start(table[:, C_B1:C_W2], io["L0_ffn_spline_b1"]).then_inc(w_table, 16)
            sp.dma_start(table[:, C_W2:C_B2], io["L0_ffn_spline_w2"].rearrange("n g o -> n (g o)")).then_inc(w_table, 16)
            sp.dma_start(table[:, C_B2:C_DIR], io["L0_ffn_spline_b2"]).then_inc(w_table, 16)
            sp.dma_start(table[:, C_DIR:C_ALL], io["L0_ffn_directions"]).then_inc(w_table, 16)
            for half in range(2):
                at, cols = slice(M * half, M * half + M), slice(HALF * half, HALF * half + HALF)
                sp.dma_start(win2[:, at], io["L1_ffn_Win"]).then_inc(w_ffn1, 16)
                sp.dma_start(bin2[at, :], column("L1_ffn_bin_")).then_inc(w_ffn1, 16)
                sp.dma_start(kw1[at, :], io["L1_ffn_W1"][:, cols]).then_inc(w_ffn1, 16)
                sp.dma_start(kb1[at, :], io["L1_ffn_b1"][:, cols]).then_inc(w_ffn1, 16)
                sp.dma_start(kw2[at, :], io["L1_ffn_W2"][:, cols]).then_inc(w_ffn1, 16)
                sp.dma_start(wout2[at, :], io["L1_ffn_Wout"]).then_inc(w_ffn1, 16)
            sp.dma_start(kb2[:, :], column("L1_ffn_b2")).then_inc(w_ffn1, 16)
            sp.dma_start(bout[:, :], row("L1_ffn_bout")).then_inc(w_ffn1, 16)

            def body(r):
                p = r.parity
                if r.k is not None or r.n < CHUNKS - 2:
                    sp.wait_ge(x_beta_ready, r.count(1, 1))
                    sp.wait_ge(xt_ps_ready, r.count(1, 1))
                    sp.dma_start(x_tok[p][:, :], x_dram[r.index(2)]).then_inc(x_loaded[p], 16)
                c = r - 4
                if c.real:
                    sp.wait_ge(o_ready, c.count(1, 1))
                    sp.dma_start(out_dram[c.index()], o_tok[p][:, :]).then_inc(out_stored[p], 16)

            run_rounds(sp, body)
            for p in range(2):
                sp.wait_ge(out_stored[p], 16 * CHUNKS // 2)

        @block.gpsimd
        def _(pool):
            nc.gpsimd.memset(ident[:, :], 0.0).then_inc(pool_step, 1)
            pool.wait_ge(pool_step, 1)
            nc.gpsimd.affine_select(out=ident[:, :], in_=ident[:, :], compare_op=ALU.not_equal, fill=1.0, base=0,
                                    pattern=[[-1, 128]], channel_multiplier=1).then_inc(ident_ready, 1)
            for l in range(2):
                nc.gpsimd.memset(gates[l][:, 4 * B:5 * B], 0.0).then_inc(const_ready, 1)
            nc.gpsimd.memset(ones3[:, :], 1.0).then_inc(const_ready, 1)
            nc.gpsimd.memset(ones1[:, :], 1.0).then_inc(const_ready, 1)
            nc.gpsimd.memset(one_hot[:, :], 0.0).then_inc(const_ready, 1)
            nc.gpsimd.memset(minus_half[:, :], -0.5).then_inc(const_ready, 1)
            for k in range(KNOTS):
                nc.gpsimd.memset(kpos[:, k:k + 1], float(k)).then_inc(const_ready, 1)
                nc.gpsimd.memset(rank[:, k:k + 1], float(NC - k)).then_inc(const_ready, 1)
            def third_part(l, c, s):
                pool.wait_ge(h_ready[l], c.count(STEPS, s + 1))
                now, p = slice(s * B, (s + 1) * B), c.parity
                nc.gpsimd.tensor_tensor(h_rest[l][:, :], h_now[l][:, :], hb[l][p][:, 0, now], ALU.subtract).then_inc(rest_ready[l], 1)
                pool.wait_ge(rest_ready[l], c.count(STEPS, s + 1))
                pool.wait_ge(part_ready[l][1], c.count(STEPS, s + 1))
                nc.gpsimd.tensor_tensor(hb[l][p][:, 2, now], h_rest[l][:, :], hb[l][p][:, 1, now],
                                        ALU.subtract).then_inc(part_ready[l][2], 1)

            def fill(r, half, after):
                p = r.parity
                c, cx = r - 1, r - 2
                if r.first and (half, after) in ((7, 1), (11, 1)):
                    pool.wait_ge(l1_scaled, 4 if half == 7 else 5)
                    if half == 7:
                        nc.gpsimd.tensor_tensor(wh[1][:, :], wh[1][:, :], whb[1][:, 0], ALU.subtract).then_inc(l1_rest, 1)
                    else:
                        nc.gpsimd.tensor_tensor(whb[1][:, 2], wh[1][:, :], whb[1][:, 1], ALU.subtract).then_inc(l1_w_ready, 1)
                if (half, after) == TILE_AT and c.real:
                    pool.wait_ge(route, c.count(ROUTE, ROUTE))
                    if not c.first:
                        pool.wait_ge(one_hot_ps_ready, c.count(1))
                    nc.gpsimd.tensor_tensor(
                        one_hot[:, 0:NT].rearrange("p (c j) -> p c j", c=NC),
                        in_cluster[:, :].unsqueeze(2).to_broadcast([TOK, NC, TPC]),
                        in_local[:, :].unsqueeze(1).to_broadcast([TOK, NC, TPC]), ALU.mult).then_inc(one_hot_ready, 1)
                if (half, after) == RSTD_AT and c.real:
                    pool.wait_ge(norm_step, c.count(4, 3))
                    nc.gpsimd.tensor_tensor(rstd[:, :], var_eps[:, :], minus_half[:, :], ALU.pow).then_inc(rstd_ready, 1)
                if (half, after) == KEEP_AT and cx.real:
                    if (r - 4).real:
                        pool.wait_ge(o_ready, (r - 4).count(1, 1))
                    if cx.first:
                        pool.wait_ge(ffn1_const_ready, 1)
                    pool.wait_ge(x1_ready, cx.count(1, 1))
                    nc.gpsimd.tensor_tensor(x1_keep[p][:, :], x1_tok[:, :], ffn1_const[:, :], ALU.add).then_inc(x1_kept, 1)
                if (half, after) == X_BETA_AT and r.real:
                    if r.first:
                        pool.wait_ge(w_ffn0, 144)
                    pool.wait_ge(x_loaded[p], r.pairs(16, 16))
                    if r.k is not None or r.n >= 2:
                        pool.wait_ge(x1_ready, r.count(1, -1))
                    nc.gpsimd.tensor_tensor(x_beta[p][:, :], x_tok[p][:, :], beta[:, :], ALU.add).then_inc(x_beta_ready, 1)

            def body(r):
                for half in range(2 * STEPS):
                    l, s = half % 2, half // 2
                    c, step_ = lstm1_step(r, s) if l else (r, s)
                    fill(r, half, 0)
                    if c.real:
                        third_part(l, c, step_)
                    fill(r, half, 1)

            run_rounds(pool, body)

        @block.tensor
        def _(pe):
            pe.wait_ge(const_ready, 6 + 2 * KNOTS)
            pe.wait_ge(bias0_row_ready, 1)
            for q, g in enumerate(GATE):
                pe.matmul(pre[0][0][:, q].rearrange("d s b -> d (s b)"), bias3[0:1, g * D:(g + 1) * D],
                          ones1[:, :], start=(q == 0), stop=False, skip_group_check=True)
            pe.wait_ge(ident_ready, 1)
            pe.wait_ge(x_loaded[0], 16)
            pe.transpose(turn_ps, x_tok[0][:, :], ident[:, :]).then_inc(xt_ps_ready, 1)
            pe.wait_ge(w_cond, 16)
            pe.transpose(ps_c[:, 0:B], cond[:, :], ident[0:B, 0:B]).then_inc(turned0, 1)

            def x_part(l, p, src, q, bias=True):
                g = GATE[q]
                bank = pre[l][p][:, q].rearrange("d s b -> d (s b)")
                if bias:
                    at = A_LSTM[l] + g * D
                    pe.matmul(bank, biasb[:, at:at + D], ones3[:, :], start=(q == 0), stop=False, skip_group_check=True)
                pe.matmul(bank, wx[l][:, g * D:(g + 1) * D], src[:, :], start=False, stop=False, skip_group_check=True)

            def h_part(l, c, s, between):
                p = c.parity
                before = slice((s - 1) * B, s * B) if s else slice(TOK - B, TOK)
                h_parts = hb[l][p if s else 1 - p]
                for part in range(3):
                    if part == 2:
                        between()
                    if c.first and s == 0:
                        pe.wait_ge(start_ready, 6)
                    else:
                        pe.wait_ge(part_ready[l][part], c.count(STEPS, s))
                    for q, g in enumerate(GATE):
                        for wp in range(3 - part):
                            mm = pe.matmul(pre[l][p][:, q, s], whb[l][:, wp, g * D:(g + 1) * D], h_parts[:, part, before],
                                           start=False, stop=True, skip_group_check=True)
                mm.then_inc(pre_ready[l], 1)

            pe.wait_ge(wx0_ready, 1)
            pe.wait_ge(xt_ready, 1)
            for q in range(4):
                x_part(0, 0, x_t[0], q, bias=False)
            pe.wait_ge(lstm0_w_ready, 1)

            def score(c, part):
                for wp in range(3 - part):
                    mm = pe.matmul(ps_a[:, 0:SCORES + CH], hb[0][c.parity][:, part, :], score_wb[:, wp, :],
                                   start=(part == 0 and wp == 0), stop=(part == 2), skip_group_check=True)
                return mm

            def turn_h(c, part):
                return pe.matmul(h_tok_ps, hb[0][c.parity][:, part, :], identb[:, :], start=(part == 0), stop=(part == 2),
                                 skip_group_check=True)

            def ffn1_in(c, part, wps):
                for wp in wps:
                    mm = pe.matmul(ps_d[:, 0:TOK], win2b[:, wp, :], hb[1][c.parity][:, part, :],
                                   start=(part == 0 and wp == 0), stop=(part == 2), skip_group_check=True)
                return mm

            def gather(c, wp):
                return pe.matmul(ps_c[:, 0:C_ALL], one_hot_t[:, :], tableb[:, wp, :], start=(wp == 0), stop=(wp == 2),
                                 skip_group_check=True)

            def between(r, half):
                c0 = r - 1
                if half in TURN_H_AT and c0.real:
                    part = TURN_H_AT.index(half)
                    if part == 0:
                        if c0.first:
                            pe.wait_ge(identb_ready, 1)
                        else:
                            pe.wait_ge(mag_step, c0.count(5))
                    turned = turn_h(c0, part)
                    if part == 2:
                        turned.then_inc(h_tok_ps_ready, 1)

            def fill(r, half):
                p = r.parity
                c0, cx, c1, c2 = r - 1, r - 2, r - 3, r - 4
                prepare = r.k is not None or r.n < CHUNKS - 1
                if half == 0 and c0.real:
                    if c0.first:
                        pe.wait_ge(score_w_ready, 1)
                    if not c0.first:
                        pe.wait_ge(gelu_ready, c0.count(1))
                    for part in range(3):
                        if not r.real:
                            pe.wait_ge(part_ready[0][part], c0.count(STEPS, STEPS))
                        scored = score(c0, part)
                        if part == 0:
                            pe.matmul(ps_a[:, SCORES:SCORES + CH], ones3[:, :], biasb[:, A_COMP:A_COMP + CH], start=False,
                                      stop=False, skip_group_check=True)
                    scored.then_inc(scores_ready, 1)
                if half == 3 and r.k is None and r.n == 1:
                    pe.wait_ge(w_ffn1, 224)
                    pe.matmul(ps_d[:, 0:D], kb2[:, :].to_broadcast([M, TOK]), wout2[0:M, :], start=True, stop=False)
                    pe.matmul(ps_d[:, 0:D], ones1[:, :], bout[:, :], start=False, stop=True).then_inc(const_ps_ready, 1)
                if half == 1 and r.first:
                    pe.wait_ge(w_ffn0, 144)
                    pe.transpose(ps_d[:, 0:NT], raw[:, :], ident[0:NT, 0:NT]).then_inc(turned0, 1)
                for c, at, bank in ((c0, half, 1 - p), (cx, half + 2 * STEPS, p)):
                    if c.real and at in L1_X_AT:
                        q = L1_X_AT.index(at)
                        if q == 0:
                            if c.first:
                                pe.wait_ge(bias1_ready, 1)
                                pe.wait_ge(l1_w_ready, 2)
                            pe.wait_ge(x1t_ready, c.count(1, 1))
                        x_part(1, bank, x1_t, q)
                if half == FFN1_END_AT and c2.real:
                    pe.wait_ge(inner_step, c2.count(HALF, HALF))
                    pe.matmul(ps_d[:, 0:D], inner[:, :], wout2[:, :], start=True, stop=True).then_inc(ffn1_ps_ready, 1)
                if half == TURN_X_AT and prepare:
                    pe.wait_ge(x_loaded[1 - p], r.pairs(16, 16 + 16 * p))
                    if cx.real:
                        pe.wait_ge(x1t_ready, cx.count(1, 1))
                    elif r.first:
                        pe.wait_ge(xt_ready, 1)
                    else:
                        pe.wait_ge(xt_ready, 2)
                    pe.transpose(turn_ps, x_tok[1 - p][:, :], ident[:, :]).then_inc(xt_ps_ready, 1)
                if half == FFN1_IN_AT[0] and c1.real:
                    if c1.first:
                        pe.wait_ge(ffn1_w_ready, 1)
                    else:
                        pe.wait_ge(o_ready, c1.count(1))
                    if not cx.real:
                        pe.wait_ge(part_ready[1][0], c1.count(STEPS, STEPS))
                    ffn1_in(c1, 0, [0, 1, 2])
                if half == FFN1_IN_AT[1] and c1.real:
                    if not cx.real:
                        pe.wait_ge(part_ready[1][1], c1.count(STEPS, STEPS))
                    ffn1_in(c1, 1, [0, 1])
                    if not cx.real:
                        pe.wait_ge(part_ready[1][2], c1.count(STEPS, STEPS))
                    ffn1_in(c1, 2, [0]).then_inc(s1_ps_ready, 1)
                if half == TURN_TILE_AT and c0.real:
                    if prepare:
                        pe.wait_ge(xt_ready, r.count(1, 2))
                    elif cx.real:
                        pe.wait_ge(x1t_ready, cx.count(1, 1))
                    pe.wait_ge(one_hot_ready, c0.count(1, 1))
                    pe.matmul(turn_ps, one_hot[:, :], identb[:, :], start=True, stop=True).then_inc(one_hot_ps_ready, 1)
                if half == GATHER_AT and c0.real:
                    if c0.first:
                        pe.wait_ge(table_ready, 1)
                    pe.wait_ge(one_hot_t_ready, c0.count(1, 1))
                    for wp in range(3):
                        gathering = gather(c0, wp)
                    gathering.then_inc(gathered, 1)
                if half in L0_X_AT and prepare:
                    q = L0_X_AT.index(half)
                    if q == 0:
                        if r.first:
                            pe.wait_ge(bias0_ready, 1)
                        pe.wait_ge(xt_ready, r.count(1, 2))
                    x_part(0, 1 - p, x_t[1 - p], q)
                if half == TURN_X1_AT and c0.real:
                    pe.wait_ge(x1_ready, c0.count(1, 1))
                    pe.transpose(turn_ps, x1_tok[:, :], ident[:, :]).then_inc(x1t_ps_ready, 1)

            def body(r):
                for s in range(STEPS):
                    if r.real:
                        h_part(0, r, s, lambda: between(r, 2 * s))
                    else:
                        between(r, 2 * s)
                    fill(r, 2 * s)
                    c, step1 = lstm1_step(r, s)
                    if c.real:
                        h_part(1, c, step1, lambda: between(r, 2 * s + 1))
                    else:
                        between(r, 2 * s + 1)
                    fill(r, 2 * s + 1)

            run_rounds(pe, body)

        @block.scalar
        def _(act):
            act.dma_start(bias3[:, 0:4 * D], row("L0_cond_b").to_broadcast([3, 4 * D])).then_inc(w_bias0, 16)
            act.dma_start(wx[0][:, :], io["L0_cond_Wx"]).then_inc(w_lstm0_x, 16)
            act.wait_ge(const_ready, 6 + 2 * KNOTS)
            nc.scalar.activation(table_load[:, :], minus_half[:, :], ACT.Gelu).then_inc(table_loaded, 1)
            act.wait_ge(xt_ps_ready, 1)
            nc.scalar.activation(x_t[0][:, :], turn_ps, ACT.Identity).then_inc(xt_ready, 1)
            act.wait_ge(w_lstm0_x, 16)
            nc.scalar.activation(wx[0][:, 0:3 * D], wx[0][:, 0:3 * D], ACT.Identity, scale=0.5).then_inc(wx0_ready, 1)
            nc.scalar.activation(identb[:, :], ident[:, :], ACT.Identity).then_inc(identb_ready, 1)

            def scale_lstm1(dst, src):
                nc.scalar.activation(dst[:, 0:3 * D], src[:, 0:3 * D], ACT.Identity, scale=0.25).then_inc(l1_scaled, 1)
                nc.scalar.activation(dst[:, 3 * D:], src[:, 3 * D:], ACT.Identity, scale=0.5).then_inc(l1_scaled, 1)

            def prepare_lstm1(half):
                if half == 3:
                    act.wait_ge(w_lstm1, 32)
                    scale_lstm1(whb[1][:, 0], wh[1])
                if half == 5:
                    scale_lstm1(wh[1], wh[1])
                if half == 7:
                    nc.scalar.activation(wx[1][:, 0:3 * D], wx[1][:, 0:3 * D], ACT.Identity, scale=0.5).then_inc(l1_w_ready, 1)
                if half == 9:
                    act.wait_ge(l1_rest, 1)
                    nc.scalar.activation(whb[1][:, 1], wh[1][:, :], ACT.Identity).then_inc(l1_scaled, 1)

            def gate_tanh(l, c, s):
                act.wait_ge(pre_ready[l], c.count(STEPS, s + 1))
                nc.scalar.activation(gates[l][:, 0:4 * B].rearrange("d (g b) -> d g b", g=4),
                                     pre[l][c.parity][:, :, s], ACT.Tanh).then_inc(gates_ready[l], 1)

            def cell_tanh_(l, c, s):
                act.wait_ge(cell_ready[l], c.count(STEPS, s + 1))
                nc.scalar.activation(cell_tanh[l][:, :], gates[l][:, 4 * B:5 * B], ACT.Tanh, scale=0.5).then_inc(tanh_ready[l], 1)

            def relu(c, j):
                if j == 0:
                    act.wait_ge(s1_ready, c.count(1, 1))
                if j == 0 and not c.first:
                    act.wait_ge(inner_step, c.count(HALF))
                nc.scalar.activation(relus[:, j, :], s1[:, :], ACT.Relu, bias=kb1[:, j:j + 1],
                                     scale=kw1[:, j:j + 1]).then_inc(relus_ready, 1)

            def fill(r, half, late):
                p, here = r.parity, (half, late)
                c0, c1, c2 = r - 1, r - 3, r - 4
                if r.first and late:
                    prepare_lstm1(half)
                if here == (4, 0) and r.k is None and r.n == 1:
                    act.wait_ge(const_ps_ready, 1)
                    nc.scalar.activation(ffn1_const[:, :], ps_d[:, 0:D], ACT.Identity).then_inc(ffn1_const_ready, 1)
                if here == TANHS_AT and c0.real:
                    if c0.first:
                        act.wait_ge(temp_ready, 1)
                    act.wait_ge(scores_ready, c0.count(1, 1))
                    nc.scalar.activation(tanhs[:, :], ps_a[:, 0:SCORES], ACT.Tanh, scale=half_inv_temp[:, :]).then_inc(tanhs_ready, 1)
                if here == GELU_AT and c0.real:
                    if not c0.first:
                        act.wait_ge(comp_summed, c0.count(2))
                    nc.scalar.activation(gelu[:, 0:CH], ps_a[:, SCORES:SCORES + CH], ACT.Gelu).then_inc(gelu_ready, 1)
                if here == X_T_AT and (r.k is not None or r.n < CHUNKS - 1):
                    act.wait_ge(xt_ps_ready, r.count(1, 2))
                    nc.scalar.activation(x_t[1 - p][:, :], turn_ps, ACT.Identity).then_inc(xt_ready, 1)
                if here == H_TOK_AT and c0.real:
                    act.wait_ge(h_tok_ps_ready, c0.count(1, 1))
                    nc.scalar.activation(h_tok[:, :], h_tok_ps, ACT.Identity).then_inc(h_tok_ready, 1)
                if here == TILE_T_AT and c0.real:
                    act.wait_ge(one_hot_ps_ready, c0.count(1, 1))
                    nc.scalar.activation(one_hot_t[:, :], ps_b[0:NT, 0:TOK], ACT.Identity).then_inc(one_hot_t_ready, 1)
                if here == SPLINE_ROW_AT and c0.real:
                    act.wait_ge(comp_summed, c0.count(2, 2))
                    nc.scalar.activation(comp[:, :], comp_sum[:, :], ACT.Tanh).then_inc(comp_ready, 1)
                    act.wait_ge(gathered, c0.count(1, 1))
                    nc.scalar.activation(spline[:, :], ps_c[:, 0:C_DIR], ACT.Identity).then_inc(spline_ready, 1)
                if here == X1_T_AT and c0.real:
                    act.wait_ge(x1t_ps_ready, c0.count(1, 1))
                    nc.scalar.activation(x1_t[:, :], turn_ps, ACT.Identity).then_inc(x1t_ready, 1)
                if here == S1_AT and c1.real:
                    act.wait_ge(s1_ps_ready, c1.count(1, 1))
                    nc.scalar.activation(s1[:, :], ps_d[:, 0:TOK], ACT.Identity, bias=bin2[:, :]).then_inc(s1_ready, 1)
                for c, at in ((c1, half), (c2, half + 2 * STEPS)):
                    if c.real and (at, late) in RELU_AT:
                        relu(c, RELU_AT.index((at, late)))

            def body(r):
                for half in range(2 * STEPS):
                    l, s = half % 2, half // 2
                    c, step = lstm1_step(r, s) if l else (r, s)
                    if c.real:
                        gate_tanh(l, c, step)
                    fill(r, half, 0)
                    if c.real:
                        cell_tanh_(l, c, step)
                    fill(r, half, 1)

            run_rounds(act, body)

        @block.vector
        def _(dve):
            count = [0]

            def done(ins):
                count[0] += 1
                ins.then_inc(set_dve, 1)
                return count[0]

            def step(ins):
                dve.wait_ge(set_dve, done(ins))

            def ready():
                dve.wait_ge(set_dve, count[0])

            ifo, g_ = slice(0, 3 * D), slice(3 * D, 4 * D)
            dve.wait_ge(w_bias0, 16)
            nc.vector.tensor_scalar(bias3[:, ifo], bias3[:, ifo], 0.5, None, ALU.mult).then_inc(bias0_row_ready, 1)
            dve.wait_ge(w_lstm0, 16)
            nc.vector.tensor_scalar(whb[0][:, 0, ifo], wh[0][:, ifo], 0.25, None, ALU.mult).then_inc(set_dve, 1)
            count[0] += 1
            first_part = done(nc.vector.tensor_scalar(whb[0][:, 0, g_], wh[0][:, g_], 0.5, None, ALU.mult))
            dve.wait_ge(set_dve, first_part)
            done(nc.vector.scalar_tensor_tensor(out=wh[0][:, ifo], in0=wh[0][:, ifo], scalar=0.25, in1=whb[0][:, 0, ifo],
                                                op0=ALU.mult, op1=ALU.subtract))
            rest_done = done(nc.vector.scalar_tensor_tensor(out=wh[0][:, g_], in0=wh[0][:, g_], scalar=0.5, in1=whb[0][:, 0, g_],
                                                            op0=ALU.mult, op1=ALU.subtract))
            dve.wait_ge(turned0, 1)
            start_done = done(nc.vector.tensor_scalar(start[:, :], ps_c[:, 0:B], 2.0, None, ALU.mult))
            last = slice(TOK - B, TOK)
            dve.wait_ge(set_dve, rest_done)
            second_part = done(nc.vector.tensor_copy(whb[0][:, 1], wh[0][:, :]))
            dve.wait_ge(set_dve, start_done)
            for l in range(2):
                nc.vector.tensor_copy(hb[l][1][:, 0, last], start[:, :]).then_inc(start_ready, 1)
            dve.wait_ge(set_dve, second_part)
            nc.vector.tensor_tensor(whb[0][:, 2], wh[0][:, :], whb[0][:, 1], ALU.subtract).then_inc(lstm0_w_ready, 1)
            for q in (1, 2):
                dve.wait_ge(start_ready, 2 * q)
                step(nc.vector.tensor_tensor(start[:, :], start[:, :], hb[0][1][:, q - 1, last], ALU.subtract))
                for l in range(2):
                    nc.vector.tensor_copy(hb[l][1][:, q, last], start[:, :]).then_inc(start_ready, 1)

            rows0, rows1 = (0, 4 * D + CH), (A_LSTM[1], A_LSTM[1] + 4 * D)

            def part_of_rows(c0_, c1_, n):
                t = slice(0, c1_ - c0_)
                ready()
                done(nc.vector.tensor_copy(bias_p[:, t], bias3[:, c0_:c1_] if n == 0 else bias_r[:, t]))

            def take_off(c0_, c1_, n):
                t = slice(0, c1_ - c0_)
                ready()
                done(nc.vector.scalar_tensor_tensor(out=bias_r[:, t], in0=bias_p[:, t], scalar=later[:, n:n + 1],
                                                    in1=bias3[:, c0_:c1_] if n == 0 else bias_r[:, t], op0=ALU.mult, op1=ALU.add))

            def last_part(c0_, c1_):
                ready()
                return nc.vector.tensor_copy(biasb[:, c0_:c1_], bias_r[:, 0:c1_ - c0_])

            def split_first(parts, rest, src):
                ready()
                done(nc.vector.tensor_copy(parts[:, 0], src[:, :]))
                ready()
                done(nc.vector.tensor_tensor(rest[:, :], src[:, :], parts[:, 0], ALU.subtract))

            def split_last(parts, rest):
                ready()
                done(nc.vector.tensor_copy(parts[:, 1], rest[:, :]))
                ready()
                return nc.vector.tensor_tensor(parts[:, 2], rest[:, :], parts[:, 1], ALU.subtract)

            tiles = sig_t[:, :].rearrange("d (c j) -> d c j", c=NC)

            def set_up(n):
                if n == 0:
                    dve.wait_ge(w_bias, 16)
                    nc.vector.tensor_scalar(later[:, 0:1], ident[0:3, 0:1], 1.0, None, ALU.subtract)
                    ready()
                    done(nc.vector.tensor_scalar(later[:, 1:2], ident[0:3, 2:3], -1.0, None, ALU.mult))
                    part_of_rows(*rows0, 0)
                if n == 1:
                    take_off(*rows0, 0)
                    part_of_rows(*rows0, 1)
                if n == 2:
                    take_off(*rows0, 1)
                    dve.wait_ge(w_ffn0, 144)
                    ready()
                    done(nc.vector.tensor_scalar(temp[:, :], temp[:, :], 1e-6, None, ALU.add))
                    ready()
                    done(nc.vector.reciprocal(half_inv_temp[:, :], temp[:, :]))
                    ready()
                    nc.vector.tensor_scalar(half_inv_temp[:, :], half_inv_temp[:, :], 0.5, None, ALU.mult).then_inc(temp_ready, 1)
                if n == 3:
                    last_part(*rows0).then_inc(bias0_ready, 1)
                    dve.wait_ge(turned0, 2)
                    ready()
                    done(nc.vector.tensor_copy(sig_raw[:, :], ps_d[:, 0:NT]))
                    ready()
                    done(nc.vector.tensor_scalar(sig_a[:, :], sig_raw[:, :], -0.3, -1.0, ALU.is_lt, ALU.mult))
                if n == 4:
                    ready()
                    done(nc.vector.scalar_tensor_tensor(out=sig_q[:, :], in0=sig_raw[:, :], scalar=0.3, in1=sig_a[:, :],
                                                        op0=ALU.is_gt, op1=ALU.add))
                    ready()
                    done(nc.vector.tensor_tensor(sig_a[:, :], sig_q[:, :], sig_raw[:, :], ALU.subtract))
                    ready()
                    done(nc.vector.tensor_tensor(sig_t[:, :], sig_raw[:, :], sig_a[:, :], ALU.add))
                    ready()
                    done(nc.vector.tensor_tensor(csum[:, 1], tiles[:, :, 0], tiles[:, :, 1], ALU.add))
                if n in (5, 6):
                    for j in range(2, 7) if n == 5 else range(7, TPC):
                        ready()
                        done(nc.vector.tensor_tensor(csum[:, j % 2], csum[:, (j + 1) % 2], tiles[:, :, j], ALU.add))
                if n == 6:
                    total = csum[:, (TPC - 1) % 2]
                    ready()
                    nc.vector.tensor_scalar(cneg[:, :], total, 0.0, 0.5, ALU.is_lt, ALU.mult)
                    nc.vector.tensor_scalar(score_w[:, NC:SCORES], sig_t[:, :], 0.5, None, ALU.mult)
                    nc.vector.tensor_scalar(score_w[:, SCORES:], score_w[:, SCORES:], 0.5, None, ALU.mult)
                    ready()
                    done(nc.vector.tensor_scalar(csum[:, TPC % 2], total, 0.0, 0.5, ALU.is_gt, ALU.mult))
                    ready()
                    done(nc.vector.tensor_tensor(score_w[:, 0:NC], csum[:, TPC % 2], cneg[:, :], ALU.subtract))
                    nc.vector.memset(slopes[:, KNOTS - 1:KNOTS], 0.0)
                    nc.vector.memset(gelu[:, CH:CH + 1], 1.0)
                    nc.vector.tensor_tensor(slopes[:, 0:KNOTS - 1], knots[:, 1:KNOTS], knots[:, 0:KNOTS - 1], ALU.subtract)
                    ready()
                    done(nc.vector.tensor_scalar(scale2[:, :], scale2[:, :], 2.0, None, ALU.mult))
                if n == 7:
                    split_first(score_wb, score_r, score_w)
                    split_last(score_wb, score_r).then_inc(score_w_ready, 1)
                if n == 8:
                    dve.wait_ge(w_table, 80)
                    split_first(tableb, table_r, table)
                if n == 9:
                    split_last(tableb, table_r).then_inc(table_ready, 1)
                if n == 10:
                    dve.wait_ge(w_bias1, 16)
                    ready()
                    done(nc.vector.tensor_scalar(bias3[:, A_LSTM[1]:A_LSTM[1] + 3 * D], bias3[:, A_LSTM[1]:A_LSTM[1] + 3 * D],
                                                 0.5, None, ALU.mult))
                if n in (11, 12):
                    part_of_rows(*rows1, n - 11)
                    take_off(*rows1, n - 11)
                if n == 13:
                    last_part(*rows1).then_inc(bias1_ready, 1)
                if n == 14:
                    dve.wait_ge(w_ffn1, 224)
                    ready()
                    done(nc.vector.tensor_scalar(win2[:, :], win2[:, :], 0.5, None, ALU.mult))
                    split_first(win2b, win2_r, win2)
                if n == 15:
                    split_last(win2b, win2_r).then_inc(ffn1_w_ready, 1)

            def lstm_mix(l, c, s):
                dve.wait_ge(gates_ready[l], c.count(STEPS, s + 1))
                nc.vector.scalar_tensor_tensor(out=mixed[l][:, :], in0=gates[l][:, B:3 * B], scalar=1.0, in1=gates[l][:, 3 * B:5 * B],
                                               op0=ALU.add, op1=ALU.mult).then_inc(mixed_ready[l], 1)

            def lstm_cell(l, c, s):
                dve.wait_ge(mixed_ready[l], c.count(STEPS, s + 1))
                nc.vector.scalar_tensor_tensor(out=gates[l][:, 4 * B:5 * B], in0=mixed[l][:, B:2 * B], scalar=0.5,
                                               in1=mixed[l][:, 0:B], op0=ALU.mult, op1=ALU.add).then_inc(cell_ready[l], 1)

            def lstm_h(l, c, s):
                dve.wait_ge(tanh_ready[l], c.count(STEPS, s + 1))
                nc.vector.scalar_tensor_tensor(out=hb[l][c.parity][:, 0, s * B:(s + 1) * B], in0=gates[l][:, 0:B], scalar=1.0,
                                               in1=cell_tanh[l][:, :], op0=ALU.add, op1=ALU.mult).then_inc(part_ready[l][0], 1)
                nc.vector.scalar_tensor_tensor(out=h_now[l][:, :], in0=gates[l][:, 0:B], scalar=1.0,
                                               in1=cell_tanh[l][:, :], op0=ALU.add, op1=ALU.mult).then_inc(h_ready[l], 1)

            def lstm_part2(l, c, s):
                dve.wait_ge(h_ready[l], c.count(STEPS, s + 1))
                now = slice(s * B, (s + 1) * B)
                nc.vector.tensor_tensor(hb[l][c.parity][:, 1, now], h_now[l][:, :], hb[l][c.parity][:, 0, now],
                                        ALU.subtract).then_inc(part_ready[l][1], 1)

            def compress_sum(c, o):
                dve.wait_ge(gelu_ready, c.count(1, 1))
                nc.vector.scalar_tensor_tensor(out=gelu_w[:, o], in0=gelu[:, :], scalar=1.0,
                                               in1=comp_w2[:, :].rearrange("p (i o) -> p o i", o=2)[:, o],
                                               op0=ALU.mult, op1=ALU.mult, accum_out=comp_sum[:, o:o + 1]).then_inc(comp_summed, 1)

            def wide(ap):
                return ap.unsqueeze(2).to_broadcast([TOK, NC, KNOTS])

            def knotwise(ap):
                return ap[:, :].unsqueeze(1).to_broadcast([TOK, NC, KNOTS])

            away3 = away[:, :].rearrange("p (c k) -> p c k", c=NC)
            seg3 = seg[:, :].rearrange("p (c k) -> p c k", c=NC)

            def calibrate(src, c, n, i):
                dve.wait_ge(route, c.count(ROUTE, n))
                if i == 0:
                    ins = nc.vector.scalar_tensor_tensor(out=away3, in0=wide(src), scalar=float(KNOTS - 1), in1=knotwise(kpos),
                                                         op0=ALU.mult, op1=ALU.subtract)
                if i == 1:
                    ins = nc.vector.tensor_tensor(seg3, away3, knotwise(slopes), ALU.mult)
                if i == 2:
                    ins = nc.vector.tensor_tensor(seg3, seg3, knotwise(knots), ALU.add)
                if i == 3:
                    ins = nc.vector.scalar_tensor_tensor(out=seg3, in0=away3, scalar=1.0, in1=seg3, op0=ALU.is_lt, op1=ALU.mult)
                if i == 4:
                    ins = nc.vector.scalar_tensor_tensor(out=seg3, in0=away3, scalar=0.0, in1=seg3, op0=ALU.is_ge, op1=ALU.mult)
                if i == 5:
                    ins = nc.vector.tensor_reduce(gate_v[:, :], seg3, AX_X, ALU.add)
                ins.then_inc(route, 1)

            def first_of_largest(dst, c, n, i):
                dve.wait_ge(route, c.count(ROUTE, n))
                if i == 0:
                    ins = nc.vector.tensor_reduce(gate_m[:, :], gate_v[:, :], AX_X, ALU.max)
                if i == 1:
                    ins = nc.vector.scalar_tensor_tensor(out=ranks[:, :], in0=gate_v[:, :], scalar=gate_m[:, :], in1=rank[:, :],
                                                         op0=ALU.is_equal, op1=ALU.mult)
                if i == 2:
                    ins = nc.vector.tensor_reduce(rank_m[:, :], ranks[:, :], AX_X, ALU.max)
                if i == 3:
                    ins = nc.vector.tensor_scalar(dst[:, :], rank[:, :], rank_m[:, :], None, ALU.is_equal)
                ins.then_inc(route, 1)

            def route_step(c, n):
                if n == 0:
                    dve.wait_ge(tanhs_ready, c.count(1, 1))
                    nc.vector.tensor_scalar(sigm[:, :], tanhs[:, :], 0.5, 0.5, ALU.mult, ALU.add).then_inc(route, 1)
                elif n < 7:
                    calibrate(sigm[:, 0:NC], c, n, n - 1)
                elif n < 11:
                    first_of_largest(in_cluster, c, n, n - 7)
                elif n == 11:
                    dve.wait_ge(route, c.count(ROUTE, 11))
                    nc.vector.tensor_tensor(sel[:, :].rearrange("p (j c) -> p c j", j=TPC),
                                            sigm[:, NC:].rearrange("p (c j) -> p c j", c=NC),
                                            in_cluster[:, :].unsqueeze(2).to_broadcast([TOK, NC, TPC]),
                                            ALU.mult).then_inc(route, 1)
                elif n == 12:
                    dve.wait_ge(route, c.count(ROUTE, 12))
                    nc.vector.tensor_reduce(picked[:, :], sel[:, :].rearrange("p (j c) -> p j c", j=TPC), AX_X,
                                            ALU.add).then_inc(route, 1)
                elif n < 19:
                    calibrate(picked[:, :], c, n, n - 13)
                else:
                    first_of_largest(in_local, c, n, n - 19)

            def inner_sum(c, j):
                dve.wait_ge(relus_ready, c.count(HALF, j + 1))
                if j == 0:
                    if not (c.k is None and c.n == 0):
                        dve.wait_ge(ffn1_ps_ready, c.count(1))
                    nc.vector.tensor_scalar(inner[:, :], relus[:, 0, :], kw2[:, 0:1], None, ALU.mult).then_inc(inner_step, 1)
                else:
                    dve.wait_ge(inner_step, c.count(HALF, j))
                    nc.vector.scalar_tensor_tensor(out=inner[:, :], in0=relus[:, j, :], scalar=kw2[:, j:j + 1], in1=inner[:, :],
                                                   op0=ALU.mult, op1=ALU.add).then_inc(inner_step, 1)

            def spline_step(c, n):
                if n == 0:
                    dve.wait_ge(spline_ready, c.count(1, 1))
                    nc.vector.scalar_tensor_tensor(out=hidden[:, :], in0=spline[:, 0:GRID], scalar=comp[:, 0:1],
                                                   in1=spline[:, C_B1:C_W2], op0=ALU.mult, op1=ALU.add).then_inc(mag_step, 1)
                if n == 1:
                    dve.wait_ge(mag_step, c.count(5, 1))
                    nc.vector.scalar_tensor_tensor(out=hidden2[:, :], in0=spline[:, GRID:2 * GRID], scalar=comp[:, 1:2],
                                                   in1=hidden[:, :], op0=ALU.mult, op1=ALU.add).then_inc(mag_step, 1)
                if n == 2:
                    dve.wait_ge(mag_step, c.count(5, 2))
                    nc.vector.scalar_tensor_tensor(out=hidden3[:, :], in0=hidden2[:, :], scalar=0.0, in1=spline[:, C_W2:C_B2],
                                                   op0=ALU.max, op1=ALU.mult, accum_out=mag[:, :]).then_inc(mag_step, 1)
                if n == 3:
                    dve.wait_ge(mag_step, c.count(5, 3))
                    nc.vector.tensor_scalar(mag2[:, :], mag[:, :], spline[:, C_B2:C_DIR], scale2[:, :],
                                            ALU.add, ALU.mult).then_inc(mag_step, 1)
                if n == 4:
                    dve.wait_ge(mag_step, c.count(5, 4))
                    nc.vector.scalar_tensor_tensor(out=y2[:, :], in0=ps_c[:, C_DIR:C_ALL], scalar=mag2[:, :], in1=h_tok[:, :],
                                                   op0=ALU.mult, op1=ALU.add).then_inc(mag_step, 1)
                if n == 5:
                    dve.wait_ge(mag_step, c.count(5, 5))
                    nc.vector.bn_stats(stats[:, :], y2[:, :]).then_inc(norm_step, 1)
                if n == 6:
                    dve.wait_ge(norm_step, c.count(4, 2))
                    nc.vector.tensor_scalar(var_eps[:, :], mean_var[:, 1:2], 4.0 * EPS_LN, None, ALU.add).then_inc(norm_step, 1)
                if n == 7:
                    nc.vector.scalar_tensor_tensor(out=centred[:, :], in0=y2[:, :], scalar=mean_var[:, 0:1], in1=gamma[:, :],
                                                   op0=ALU.subtract, op1=ALU.mult).then_inc(norm_step, 1)
                if n == 8:
                    dve.wait_ge(norm_step, c.count(4, 4))
                    dve.wait_ge(rstd_ready, c.count(1, 1))
                    nc.vector.scalar_tensor_tensor(out=x1_tok[:, :], in0=centred[:, :], scalar=rstd[:, :],
                                                   in1=x_beta[c.parity][:, :], op0=ALU.mult, op1=ALU.add).then_inc(x1_ready, 1)

            def fill(r, half, which):
                c0, c1, c2 = r - 1, r - 3, r - 4
                for c, at in ((c1, half), (c2, half + 2 * STEPS)):
                    for j in steps_at(INNER_AT, at, which):
                        if c.real:
                            inner_sum(c, j)
                if (half, which) == OUT_AT and c2.real:
                    if c2.first:
                        dve.wait_ge(x1_kept, 1)
                    dve.wait_ge(ffn1_ps_ready, c2.count(1, 1))
                    if (r - 6).real:
                        dve.wait_ge(out_stored[r.parity], c2.pairs(16))
                    nc.vector.tensor_tensor(o_tok[r.parity][:, :], ps_d[:, 0:D], x1_keep[r.parity][:, :], ALU.add).then_inc(o_ready, 1)
                if c0.real:
                    for n in steps_at(ROUTE_AT, half, which):
                        if n < ROUTE:
                            route_step(c0, n)
                        else:
                            compress_sum(c0, n - ROUTE)
                    for n in steps_at(SPLINE_AT, half, which):
                        spline_step(c0, n)

            def body(r):
                for half in range(2 * STEPS):
                    l, s = half % 2, half // 2
                    c, step_ = lstm1_step(r, s) if l else (r, s)
                    c0 = r - 1
                    if c.real:
                        lstm_mix(l, c, step_)
                    if r.k is None and r.n < 2 and l:
                        set_up(STEPS * r.n + s)
                    fill(r, half, 0)
                    if half == AGGREGATE_AT and c0.real:
                        dve.wait_ge(norm_step, c0.count(4, 1))
                    if c.real:
                        lstm_cell(l, c, step_)
                    if half == AGGREGATE_AT and c0.real:
                        nc.vector.bn_aggr(mean_var[:, :], stats[:, :]).then_inc(norm_step, 1)
                    fill(r, half, 1)
                    if c.real:
                        lstm_h(l, c, step_)
                    fill(r, half, 2)
                    if c.real:
                        lstm_part2(l, c, step_)
                    fill(r, half, 3)

            run_rounds(dve, body)


_INS = ['x', 'cond_1024', 'L0_cond_Wx', 'L0_cond_Wh', 'L0_cond_b', 'L0_ffn_signatures_raw', 'L0_ffn_knot_values',
        'L0_ffn_temperature', 'L0_ffn_compress_w1', 'L0_ffn_compress_b1', 'L0_ffn_compress_w2', 'L0_ffn_compress_b2',
        'L0_ffn_spline_w1', 'L0_ffn_spline_b1', 'L0_ffn_spline_w2', 'L0_ffn_spline_b2', 'L0_ffn_directions',
        'L0_ffn_norm_gamma', 'L0_ffn_norm_beta', 'L0_ffn_output_scale', 'L1_cond_Wx', 'L1_cond_Wh', 'L1_cond_b',
        'L1_ffn_Win', 'L1_ffn_bin_', 'L1_ffn_W1', 'L1_ffn_b1', 'L1_ffn_W2', 'L1_ffn_b2', 'L1_ffn_Wout', 'L1_ffn_bout']


def kernel(**inputs):
    import numpy as _np
    import concourse.bacc as _bacc
    from concourse import mybir as _mybir
    from concourse.bass_utils import run_bass_kernel_spmd as _run

    nc = _bacc.Bacc("TRN2", target_bir_lowering=False, num_devices=1)
    arrays, io = {}, {}
    for name in _INS:
        a = _np.ascontiguousarray(inputs[name])
        arrays[f"in_{name}"] = a
        io[name] = nc.dram_tensor(f"in_{name}", a.shape, _mybir.dt.from_np(a.dtype), kind="ExternalInput").ap()
    out = nc.dram_tensor("out_x", (B, T, D), _mybir.dt.float32, kind="ExternalOutput").ap()
    build(nc, io, out)
    r = _run(nc, [arrays], core_ids=[0])
    return r.results[0]["out_x"]
```
